# Optimizing a Trainium2 kernel written in Bass

```python
import numpy as np
import jax
import jax.numpy as jnp

def _softmax(x, axis=-1):
    return jax.nn.softmax(x, axis=axis)

def _gelu(x):
    return jax.nn.gelu(x, approximate=True)

def _silu(x):
    return jax.nn.silu(x)

def _sigmoid(x):
    return jax.nn.sigmoid(x)

def _layernorm(x, axis=-1, eps=1e-05):
    m = jnp.mean(x, axis=axis, keepdims=True)
    v = jnp.var(x, axis=axis, keepdims=True)
    return (x - m) / jnp.sqrt(v + eps)

def _scatter_add(tgt, idx, src, axis=0):
    return tgt.at[idx].add(src)

def _segment_sum(src, seg, n):
    return jax.ops.segment_sum(src, seg, n)
kernel_name = 'mk_prb_d1_jaxref_r8_29ecdc'

def setup_inputs(seed: int=0):
    np.random.seed(seed)
    _w = jnp.asarray

    def _L0_attn_setup():
        import jax, jax.numpy as jnp
        import numpy as np
        B, T, C, H = (2, 256, 128, 16)
        D = C // H

        def _alibi_slopes(n_heads):
            return 2.0 ** (-(8.0 / n_heads) * jnp.arange(1, n_heads + 1, dtype=jnp.float32))
        key = jax.random.key(seed)
        k1, k2, k3 = jax.random.split(key, 3)
        return {'x': jax.random.normal(k1, (B, T, C), dtype=jnp.float32), 'w_attn': jax.random.normal(k2, (C, 3 * C), dtype=jnp.float32) * 0.02, 'b_attn': jnp.zeros((3 * C,), dtype=jnp.float32), 'w_proj': jax.random.normal(k3, (C, C), dtype=jnp.float32) * 0.02, 'b_proj': jnp.zeros((C,), dtype=jnp.float32)}
    _L0_attn_in = _L0_attn_setup()

    def _L0_ffn_setup():
        import jax, jax.numpy as jnp
        import numpy as np
        E, H, I = (8, 128, 512)
        B, S = (4, 256)
        key = jax.random.key(seed)
        k0, k1, k2, k3 = jax.random.split(key, 4)
        s = 0.02
        return {'hidden_states': jax.random.normal(k0, (B, S, H), dtype=jnp.float32), 'w1': jax.random.normal(k1, (E, H, I), dtype=jnp.float32) * s, 'b1': jnp.zeros((E, I), dtype=jnp.float32), 'w2': jax.random.normal(k2, (E, I, H), dtype=jnp.float32) * s, 'b2': jnp.zeros((E, H), dtype=jnp.float32), 'wr': jax.random.normal(k3, (H, E), dtype=jnp.float32) * s, 'br': jnp.zeros((E,), dtype=jnp.float32)}
    _L0_ffn_in = _L0_ffn_setup()
    _d = {'L0_attn_x': _L0_attn_in['x'], 'L0_attn_w_attn': _L0_attn_in['w_attn'], 'L0_attn_b_attn': _L0_attn_in['b_attn'], 'L0_attn_w_proj': _L0_attn_in['w_proj'], 'L0_attn_b_proj': _L0_attn_in['b_proj'], 'L0_ffn_w1': _L0_ffn_in['w1'], 'L0_ffn_b1': _L0_ffn_in['b1'], 'L0_ffn_w2': _L0_ffn_in['w2'], 'L0_ffn_b2': _L0_ffn_in['b2'], 'L0_ffn_wr': _L0_ffn_in['wr'], 'L0_ffn_br': _L0_ffn_in['br']}
    _x0 = _d['L0_attn_x']
    _d['L0_attn_x'] = jax.random.normal(jax.random.fold_in(jax.random.key(seed), 1), (8, 512, 128), dtype=_x0.dtype)
    del _x0
    return _d

def reference(L0_attn_x, L0_attn_w_attn, L0_attn_b_attn, L0_attn_w_proj, L0_attn_b_proj, L0_ffn_w1, L0_ffn_b1, L0_ffn_w2, L0_ffn_b2, L0_ffn_wr, L0_ffn_br):

    def _L0_attn_ref(x, w_attn, b_attn, w_proj, b_proj):
        import jax, jax.numpy as jnp
        import numpy as np
        B, T, C, H = (2, 256, 128, 16)
        D = C // H

        def _alibi_slopes(n_heads):
            return 2.0 ** (-(8.0 / n_heads) * jnp.arange(1, n_heads + 1, dtype=jnp.float32))
        b, t, c = x.shape
        qkv = (x @ w_attn + b_attn).reshape(b, t, 3, H, D).transpose(2, 0, 3, 1, 4)
        q, k, v = (qkv[0], qkv[1], qkv[2])
        scores = jnp.einsum('bhtd,bhsd->bhts', q, k) / jnp.sqrt(jnp.float32(D))
        slopes = _alibi_slopes(H)
        pos = jnp.arange(t, dtype=scores.dtype)
        scores = scores + slopes[None, :, None, None] * pos[None, None, None, :]
        causal = jnp.tril(jnp.ones((t, t), dtype=bool))
        scores = jnp.where(causal[None, None], scores, -jnp.inf)
        attn = jax.nn.softmax(scores, axis=-1)
        y = jnp.einsum('bhts,bhsd->bhtd', attn, v)
        y = y.transpose(0, 2, 1, 3).reshape(b, t, c)
        return y @ w_proj + b_proj

    def _L0_ffn_ref(hidden_states, w1, b1, w2, b2, wr, br):
        import jax, jax.numpy as jnp
        import numpy as np
        E, H, I = (8, 128, 512)
        B, S = (4, 256)
        b, s, h = hidden_states.shape
        x = hidden_states.reshape(-1, h)
        logits = x @ wr + br
        probs = jax.nn.softmax(logits, axis=-1)
        top_p, top_i = jax.lax.top_k(probs, 2)
        gate = top_p[:, 0] / (top_p[:, 0] + top_p[:, 1])
        top1 = top_i[:, 0]
        out = jnp.zeros_like(x)
        n_experts = w1.shape[0]
        for e in range(n_experts):
            hmid = jax.nn.gelu(x @ w1[e] + b1[e], approximate=False)
            hout = hmid @ w2[e] + b2[e]
            mask = top1 == e
            out = out + jnp.where(mask[:, None], hout * gate[:, None], 0.0)
        return out.reshape(b, s, h)
    x = L0_attn_x
    xn = _layernorm(x, axis=-1)
    x = x + _L0_attn_ref(xn, L0_attn_w_attn, L0_attn_b_attn, L0_attn_w_proj, L0_attn_b_proj) + _L0_ffn_ref(xn, L0_ffn_w1, L0_ffn_b1, L0_ffn_w2, L0_ffn_b2, L0_ffn_wr, L0_ffn_br)
    return x

_drawn_inputs = setup_inputs


def setup_inputs(seed=0):
    import zlib

    import numpy as np

    out = dict(_drawn_inputs(seed))
    spreads = {'L0_attn_b_attn': (0.0, 0.382),
     'L0_attn_b_proj': (0.0, 0.1),
     'L0_ffn_b1': (0.0, 0.631),
     'L0_ffn_b2': (0.0, 0.1),
     'L0_ffn_br': (0.0, 0.1)}
    factors = {'L0_attn_w_attn': 3.866}
    for name, (base, spread) in spreads.items():
        noise = np.random.default_rng([zlib.crc32(name.encode()), seed]).standard_normal(out[name].shape)
        drawn = base * np.exp(spread * noise) if base else spread * noise
        out[name] = jnp.asarray(drawn.astype(out[name].dtype))
    for name, factor in factors.items():
        out[name] = (out[name] * factor).astype(out[name].dtype)
    return out
```

```python
from contextlib import ExitStack

import concourse.bass as bass
from concourse import mybir

F32 = mybir.dt.float32
BF16 = mybir.dt.bfloat16
U16 = mybir.dt.uint16
U32 = mybir.dt.uint32
I32 = mybir.dt.int32
ALU = mybir.AluOpType
ACT = mybir.ActivationFunctionType
AX_X = mybir.AxisListType.X

P = 128
NB = 8
T = 512
C = 128
H = 16
D = C // H
TB = T // P
NT = NB * TB
E = 8
I = 512
IC = I // P
NST = NT + E - 1
EPS = 1e-5
BIG = 1e30
Q_SCALE = float(D) ** -0.5

W1_AT, B1_AT, W2_AT, B2_AT = 0, I, I + IC, I + IC + IC * C
WCOLS = B2_AT + C
FR = 3

PARTS_Q = (0, 0, 0, 1, 1, 2)
PARTS_K = (0, 1, 2, 0, 1, 0)
N_PROD = len(PARTS_Q) * D
N_ALIBI = 3
CM = T // 64
N_SCORE = N_PROD + N_ALIBI + CM
N_STACK = N_SCORE + 3

G = 4
NG = H // G
VW = D + 1


def score_chunks():
    out = []
    for g in range(NG):
        for sb in range(TB):
            nh = {0: 1, 1: 1, 2: 2, 3: 4}[sb]
            out += [(g, sb, h0, nh) for h0 in range(0, G, nh)]
    return out


def max_units():
    out = []
    for g in range(NG):
        out += [(3, 4 * g, 2), (3, 4 * g + 2, 2), (2, 4 * g, 2), (2, 4 * g + 2, 2), (1, 4 * g, 4)]
        if g % 2:
            out.append((0, 4 * g - 4, 8))
    return out


CHUNKS = score_chunks()
UNITS = max_units()
NC_ = len(CHUNKS)
NU = len(UNITS)
LAST_CHUNK = {}
for _n, (_g, _sb, _h, _nh) in enumerate(CHUNKS):
    LAST_CHUNK[(_g, _sb)] = _n + 1

P_AT = [G * sum(T - P * n for n in range(sb_)) for sb_ in range(TB)]
P_COLS = P_AT[-1] + G * P

UNITS_BY = [min(NU, -(-NU * (k + 1) // 13)) for k in range(NG * TB)]
STACK_DMAS = 7

ST_RING, P_RING, S_RING, Y_RING = 2, TB, 2, 2
ONE = 1


def block_kernel(nc, x, w_attn, b_attn, w_proj, b_proj, w1, b1, w2, b2, wr, br,
                 c_ident, c_bf, c_stack_q, c_stack_k, out):
    with ExitStack() as ctx:
        def sb(name, shape, dt=F32):
            return ctx.enter_context(nc.sbuf_tensor(name, shape, dt))

        def sem(name):
            return ctx.enter_context(nc.semaphore(name))

        xs_dram = nc.dram_tensor("xs_sorted", (NST * P, C), F32, kind="Internal").ap()
        ys_dram = nc.dram_tensor("ys_sorted", (NST * P, C), F32, kind="Internal").ap()
        parts_dram = nc.dram_tensor("qk_parts", (2, 2, 3, D, H, T), BF16, kind="Internal").ap()
        guard_dram = nc.dram_tensor("guard_parts", (3, H, T), BF16, kind="Internal").ap()

        xt = sb("xt", [P, NT, C])
        xn = sb("xn", [P, NT, C])
        xnT = sb("xnT", [P, NT * P])
        wall = sb("wall", [P, E, WCOLS])
        wcur = sb("wcur", [P, FR, WCOLS])
        stack = sb("stack", [P, 2, H, T], BF16)
        probs = sb("probs", [P, P_COLS])
        vt = sb("vt", [P, 2, TB, H, VW])
        xc = sb("xc", [P, 2, T])
        qkf = sb("qkf", [P, 2, T])
        qkr = sb("qkr", [P, 2, T])
        qkp = sb("qkp", [P, 2, 3, T], BF16)
        yn = sb("yn", [P, TB, C])
        yn2 = sb("yn2", [P, T])
        rcp = sb("rcp", [P, TB, G])
        mx = sb("mx", [P, TB, H])
        guard = sb("guard", [H, T])
        guard_r = sb("guard_r", [H, T])
        guard_p = sb("guard_p", [H, 3, T], BF16)
        reuse = xn[:].rearrange("p (b q n) c -> p b q n c", b=4, q=2)
        ysg, base, outb, yTq = (reuse[:, n] for n in range(4))
        yTs = yTq.rearrange("p q n c -> p q (n c)")
        slot_cur = sb("slot_cur", [P, 2, TB], U32)
        xst = sb("xst", [P, FR, C])
        xsT = sb("xsT", [P, FR, P])
        hid = sb("hid", [P, FR, IC, P])
        yst = sb("yst", [P, FR, C])
        wqkv = sb("wqkv", [P, 3 * C])
        wqk_dh = sb("wqk_dh", [P, 2, C])
        wpj = sb("wpj", [P, C])
        wrt = sb("wrt", [P, E])
        bqk = sb("bqk", [P, 2])
        bqk_s = sb("bqk_s", [P, 2])
        bvb = sb("bvb", [P, C])
        bpb = sb("bpb", [P, C])
        brb = sb("brb", [P, E])
        b1r = sb("b1r", [E * IC, P])
        ident = sb("ident", [P, P])
        cbf = sb("cbf", [P, 4, P], BF16)
        ident_b, mask_b, tri_b, ones_b = (cbf[:, n, :] for n in range(4))
        bst = sb("bst", [P, NT, 6])
        mv = sb("mv", [P, NT, 2])
        std = sb("std", [P, NT])
        rstd = sb("rstd", [P, NT])
        eps = sb("eps", [P, 1])
        tmp = wcur[:].rearrange("p r w -> p (r w)")
        lg, lg2, eqw, oh = (tmp[:, n * NT * E:(n + 1) * NT * E].rearrange("p (n e) -> p n e", e=E) for n in range(4))
        cnt, csum, rank_f = (tmp[:, n * NT * E:(n + 1) * NT * E] for n in range(4, 7))
        rank = rank_f.rearrange("p (e n) -> p e n", e=E)
        cmp = tmp[:, 7 * NT * E:7 * NT * E + NST * E].rearrange("p (j e) -> p j e", e=E)
        ohb = sb("ohb", [P, NT, E], BF16)
        w8 = sb("w8", [P, E])
        mx1 = sb("mx1", [P, NT])
        mxw = sb("mxw", [P, NT])
        mx2 = sb("mx2", [P, NT])
        dgap = sb("dgap", [P, NT])
        gexp = sb("gexp", [P, NT])
        gate = sb("gate", [P, NT])
        ones_f = sb("ones_f", [P, E * NT])
        bef = sb("bef", [P, E + 1])
        npe = sb("npe", [P, E])
        npi = sb("npi", [P, E], I32)
        nti = sb("nti", [P, E], I32)
        ntl = sb("ntl", [P, E])
        tinc = sb("tinc", [P, E])
        tex = sb("tex", [P, E])
        dlt = sb("dlt", [P, E])
        slotf = sb("slotf", [P, NT])
        slot = sb("slot", [P, NT], U32)
        jj = sb("jj", [P, NST])
        ef = sb("ef", [P, NST])
        eidx = sb("eidx", [P, NST], I32)

        ps = ctx.enter_context(nc.psum_tensor("ps", [P, 8, T], F32))
        S_BANK = (0, 2)
        ST_BANK = (4, 5)
        PV_BANK, MISC = 6, 7

        x_loaded = [sem(f"x_loaded{b}") for b in range(NB)]
        small_loaded = sem("small_loaded")
        const_loaded = sem("const_loaded")
        rows_loaded = sem("rows_loaded")
        w1_loaded = sem("w1_loaded")
        zero_made = sem("zero_made")
        zero_stored = sem("zero_stored")
        consts_made = sem("consts_made")
        iotas_made = sem("iotas_made")
        dve_chain = sem("dve_chain")
        stats_done = sem("stats_done")
        std_done = sem("std_done")
        xn_done = sem("xn_done")
        xnT_ps = sem("xnT_ps")
        xnT_done = sem("xnT_done")
        b1_ps = sem("b1_ps")
        b1_done = sem("b1_done")
        logits_ps = sem("logits_ps")
        onehot_done = sem("onehot_done")
        count_ps = sem("count_ps")
        gap_done = sem("gap_done")
        gexp_done = sem("gexp_done")
        gate_done = sem("gate_done")
        slots_done = sem("slots_done")
        experts_known = sem("experts_known")
        scattered = sem("scattered")
        bias_scaled = sem("bias_scaled")
        xs_loaded = [sem(f"xs_loaded{r}") for r in range(FR)]
        wcur_done = sem("wcur_done")
        xsT_ps = sem("xsT_ps")
        xsT_done = sem("xsT_done")
        hid_ps = sem("hid_ps")
        hid_done = sem("hid_done")
        ye_ps = sem("ye_ps")
        ye_done = sem("ye_done")
        ys_stored = [sem(f"ys_stored{r}") for r in range(FR)]
        wqk_done = sem("wqk_done")
        xc_done = sem("xc_done")
        qk_ps = sem("qk_ps")
        qk_copied = sem("qk_copied")
        qk_split = sem("qk_split")
        parts_stored = sem("parts_stored")
        stack_loaded = [[sem(f"stack_loaded{p}_{g}") for g in range(NG)] for p in range(2)]
        v_ps = sem("v_ps")
        v_done = sem("v_done")
        s_ps = sem("s_ps")
        mx_done = sem("mx_done")
        guard_ps = sem("guard_ps")
        guard_neg = sem("guard_neg")
        guard_split = sem("guard_split")
        guard_chain = sem("guard_chain")
        pool_passed = sem("pool_passed")
        guard_stored = sem("guard_stored")
        split_chain = sem("split_chain")
        guard_loaded = sem("guard_loaded")
        st_ps = sem("st_ps")
        exp_done = sem("exp_done")
        p_masked = sem("p_masked")
        pv_done = sem("pv_done")
        yT_copied = sem("yT_copied")
        yT_back = sem("yT_back")
        rcp_done = sem("rcp_done")
        y_norm = sem("y_norm")
        y2_ps = sem("y2_ps")
        y2_copied = sem("y2_copied")
        proj_ps = sem("proj_ps")
        idx_copied = sem("idx_copied")
        gathered = [sem(f"gathered{p}") for p in range(2)]
        gated = sem("gated")
        biased = sem("biased")
        base_done = sem("base_done")
        out_done = sem("out_done")
        out_stored = [sem(f"out_stored{p}") for p in range(2)]

        N_SMALL, N_CONST, N_ROWS = 9, 2, 4

        def slots(eng, body):
            with eng.Fori(0, (NB - 2) // 2) as i:
                for par in range(2):
                    body(2 * i + par, i, par, True, True)
            for b in (NB - 2, NB - 1):
                body(b, b // 2, b % 2, b + 1 < NB, False)

        def sorted_tiles(eng, body):
            for r in range(FR):
                body(0, r)
            with eng.Fori(1, NST // FR - 1) as q:
                for r in range(FR):
                    body(q, r)
            for r in range(FR):
                body(NST // FR - 1, r)

        def first(q):
            return isinstance(q, int) and q == 0

        def final(q):
            return isinstance(q, int) and q == NST // FR - 1

        block = ctx.enter_context(nc.Block())

        @block.sync
        def _(sp):
            for par in range(2):
                sp.sem_inc(out_stored[par], 16 * ONE)
            for b in range(NB):
                sp.dma_start(xt[:, TB * b:TB * (b + 1), :],
                             x[b].rearrange("(n p) c -> p n c", p=P)).then_inc(x_loaded[b], 16)
            for par in range(2):
                at = 64 * par
                sp.dma_start(stack[at + N_PROD:at + N_SCORE, 0].bitcast(U16), c_stack_q).then_inc(rows_loaded, 16)
                sp.dma_start(stack[at + N_PROD:at + N_STACK, 1].bitcast(U16), c_stack_k).then_inc(rows_loaded, 16)
            sp.wait_ge(zero_made, 1)
            zeros = probs[:, 0:NST * C]
            sp.dma_start(xs_dram.rearrange("(p n) c -> p (n c)", p=P), zeros).then_inc(zero_stored, 16)

            def store_parts(b, par):
                sp.wait_ge(qk_split, b + 1)
                for s in range(2):
                    sp.dma_start(parts_dram[par, s].rearrange("j d h t -> (d h) j t"),
                                 qkp[:, s]).then_inc(parts_stored, 16)
                sp.wait_ge(parts_stored, 32 * b + 32)

            def load_stack(par, g):
                hs = slice(G * g, G * (g + 1))
                at = 64 * par

                def one(s, row, first_part, n_parts):
                    dst = stack[at + D * row:at + D * (row + n_parts), s, hs, :]
                    src = parts_dram[par, s, first_part:first_part + n_parts, :, hs, :]
                    sp.dma_start(dst, src.rearrange("j d h t -> (j d) h t")).then_inc(stack_loaded[par][g], 16)
                for s, parts in ((0, PARTS_Q), (1, PARTS_K)):
                    row = 0
                    while row < len(parts):
                        n = 1
                        while row + n < len(parts) and parts[row + n] == parts[row] + n:
                            n += 1
                        one(s, row, parts[row], n)
                        row += n

            def load_guard(b, par):
                sp.wait_ge(guard_split, b + 1)
                sp.dma_start(guard_dram.rearrange("j h t -> h j t"), guard_p[:]).then_inc(guard_stored, 16)
                sp.wait_ge(guard_stored, 16 * b + 16)
                row = 64 * par + N_SCORE
                sp.dma_start(stack[row:row + 3, 0, :, :], guard_dram).then_inc(guard_loaded, 16)

            for b in range(2):
                store_parts(b, b)
                if b == 0:
                    sp.wait_ge(rows_loaded, 16 * N_ROWS)
                for g in range(NG):
                    load_stack(b, g)
            load_guard(0, 0)
            sp.wait_ge(scattered, 16 * NT)

            def load_tile(q, r):
                if not first(q):
                    sp.wait_ge(xsT_ps, FR * (q - 1) + r + 1)
                sp.dma_start(xst[:, r, :], xs_dram[bass.ds((FR * q + r) * P, P), :]).then_inc(xs_loaded[r], 16)

            def store_tile(q, r):
                sp.wait_ge(ye_done, FR * q + r + 1)
                sp.dma_start(ys_dram[bass.ds((FR * q + r) * P, P), :], yst[:, r, :]).then_inc(ys_stored[r], 16)

            def tile_io(q, r):
                load_tile(q, r)
                if not (first(q) and r < 2):
                    store_tile(q if r == 2 else q - 1, r - 2 if r == 2 else r + 1)

            sorted_tiles(sp, tile_io)
            for r in range(FR - 2, FR):
                store_tile(NST // FR - 1, r)

            def slot_io(b, half, par, more, steady):
                if steady:
                    store_parts(b + 2, par)
                    for g in range(NG - 1):
                        sp.wait_ge(st_ps, NC_ * b + LAST_CHUNK[(g, TB - 1)])
                        load_stack(par, g)
                if more:
                    load_guard(b + 1, 1 - par)
                if steady:
                    sp.wait_ge(st_ps, NC_ * b + NC_)
                    load_stack(par, NG - 1)
                sp.wait_ge(out_done, ONE + b + 1)
                dst = out[bass.ds(b, 1), :, :].rearrange("o (n p) c -> p (o n) c", p=P)
                sp.dma_start(dst, outb[:, par]).then_inc(out_stored[par], 16)

            slots(sp, slot_io)
            for par in range(2):
                sp.wait_ge(out_stored[par], 16 * (ONE + NB // 2))

        @block.scalar
        def _(act):
            act.dma_start(ident[:], c_ident).then_inc(const_loaded, 16)
            act.dma_start(cbf[:].bitcast(U16), c_bf).then_inc(const_loaded, 16)
            act.dma_start(wrt[:], wr).then_inc(small_loaded, 16)
            act.dma_start(wqkv[:], w_attn).then_inc(small_loaded, 16)
            for s in range(2):
                act.dma_start(bqk[:, s:s + 1], b_attn[s * C:(s + 1) * C].rearrange("(h d o) -> d h o", d=D, o=1),
                              allow_slow_non_contiguous=True).then_inc(small_loaded, 16)
            act.dma_start(bvb[:], b_attn[2 * C:3 * C].partition_broadcast(P)).then_inc(small_loaded, 16)
            act.dma_start(bpb[:], b_proj.partition_broadcast(P)).then_inc(small_loaded, 16)
            act.dma_start(brb[:], br.partition_broadcast(P)).then_inc(small_loaded, 16)
            act.dma_start(b1r[:], b1.rearrange("e (i p) -> (e i) p", p=P)).then_inc(small_loaded, 16)
            act.dma_start(wpj[:], w_proj).then_inc(small_loaded, 16)
            for e in range(E):
                act.dma_start(wall[:, e, W1_AT:W1_AT + I], w1[e]).then_inc(w1_loaded, 16)
                act.dma_start(wall[:, e, W2_AT:W2_AT + IC * C].rearrange("p (i c) -> p i c", i=IC),
                              w2[e].rearrange("(i p) c -> p i c", p=P)).then_inc(w1_loaded, 16)
                act.dma_start(wall[:, e, B2_AT:B2_AT + C], b2[e].partition_broadcast(P)).then_inc(w1_loaded, 16)

            act.sem_inc(exp_done, ST_RING)
            act.sem_inc(yT_copied, ONE)
            for b in range(NB + 2):
                if b < NB:
                    act.wait_ge(stats_done, b + 1)
                    act.activation(std[:, TB * b:TB * (b + 1)], mv[:, TB * b:TB * (b + 1), 1], ACT.Sqrt,
                                   bias=eps[:]).then_inc(std_done, 1)
                b -= 2
                if b < 0:
                    continue
                act.wait_ge(xnT_ps, b + 1)
                act.copy(xnT[:, b * T:(b + 1) * T], ps[:, b % 2, :]).then_inc(xnT_done, 1)
            act.wait_ge(b1_ps, 1)
            act.copy(wall[:, :, B1_AT:B1_AT + IC], ps[:, 3, 0:E * IC].rearrange("p (e i) -> p e i", e=E)
                     ).then_inc(b1_done, 1)
            act.wait_ge(small_loaded, 16 * N_SMALL)
            act.mul(bqk_s[:, 0:1], bqk[:, 0:1], Q_SCALE).then_inc(bias_scaled, 1)
            act.copy(bqk_s[:, 1:2], bqk[:, 1:2]).then_inc(bias_scaled, 1)
            act.wait_ge(bias_scaled, 2)

            def copy_qk(b):
                if not (isinstance(b, int) and b == 0):
                    act.wait_ge(qk_split, b)
                for s in range(2):
                    act.wait_ge(qk_ps, 2 * b + s + 1)
                    act.activation(qkf[:, s, :], ps[:, MISC, :], ACT.Identity, bias=bqk_s[:, s:s + 1],
                                   scale=Q_SCALE if s == 0 else 1.0).then_inc(qk_copied, 1)

            copy_qk(0)
            copy_qk(1)
            act.wait_ge(gap_done, 1)
            act.activation(gexp[:], dgap[:], ACT.Exp).then_inc(gexp_done, 1)

            def tile_act(q, r):
                n = FR * q + r
                act.wait_ge(xsT_ps, n + 1)
                if not first(q):
                    act.wait_ge(hid_ps, n - FR + 1)
                act.copy(xsT[:, r, :], ps[:, r, 0:P]).then_inc(xsT_done, 1)

            def tile_gelu(q, r):
                n = FR * q + r
                act.wait_ge(hid_ps, n + 1)
                if not first(q):
                    act.wait_ge(ye_ps, n - FR + 1)
                for i in range(IC):
                    last = act.activation(hid[:, r, i, :], ps[:, 3 + r, i * P:(i + 1) * P], ACT.Gelu,
                                          bias=wcur[:, r, B1_AT + i:B1_AT + i + 1])
                last.then_inc(hid_done, 1)

            def tile_pair(q, r):
                if not (final(q) and r == FR - 1):
                    tile_act(q + 1 if r == FR - 1 else q, (r + 1) % FR)
                tile_gelu(q, r)

            tile_act(0, 0)
            sorted_tiles(act, tile_pair)

            act.wait_ge(zero_stored, 16)

            def slot_act(b, half, par, more, steady):
                def exps(k):
                    g, sb_ = divmod(k, TB)
                    w = T - P * sb_
                    act.wait_ge(pv_done, NG * TB * b + k + 1)
                    for n, (cg, csb, h0, nh) in enumerate(CHUNKS):
                        if (cg, csb) != (g, sb_):
                            continue
                        act.wait_ge(st_ps, NC_ * b + n + 1)
                        at = P_AT[sb_] + h0 * w
                        act.activation(probs[:, at:at + nh * w].rearrange("p (h w) -> p h w", h=nh),
                                       ps[:, ST_BANK[n % 2], 0:nh * w].rearrange("p (h w) -> p h w", h=nh),
                                       ACT.Exp).then_inc(exp_done, 1)

                def copy_yT(g):
                    act.wait_ge(pv_done, P_RING + NG * TB * b + TB * g + TB)
                    act.wait_ge(yT_back, NG * b + g + 1)
                    act.copy(yTs[:, g % 2, :], ps[:, PV_BANK, :]).then_inc(yT_copied, 1)

                for k in range(NG * TB):
                    exps(k)
                    if k == 2 and steady:
                        copy_qk(b + 2)
                    if k % TB == 0 and k:
                        copy_yT(k // TB - 1)
                copy_yT(NG - 1)
                act.wait_ge(proj_ps, b + 1)
                act.wait_ge(y2_ps, ONE + b + 1)
                act.copy(yn2[:], ps[:, MISC, :]).then_inc(y2_copied, 1)

            slots(act, slot_act)

        @block.vector
        def _(dve):
            chain = [0]

            def then(ins):
                chain[0] += 1
                ins.then_inc(dve_chain, 1)
                dve.wait_ge(dve_chain, chain[0])

            dve.memset(ones_f[:], 1.0)
            dve.memset(bef[:, 0:1], 0.0)
            dve.memset(eps[:], EPS)
            dve.memset(ps[:, PV_BANK, :], 0.0)
            dve.memset(vt[:], 1.0).then_inc(consts_made, 1)
            dve.sem_inc(mx_done, S_RING)
            dve.sem_inc(out_done, ONE)

            def normalise(b):
                dve.wait_ge(std_done, b + 1)
                then(dve.reciprocal(rstd[:, TB * b:TB * (b + 1)], std[:, TB * b:TB * (b + 1)]))
                for t in range(TB * b, TB * (b + 1)):
                    last = dve.tensor_scalar(xn[:, t, :], xt[:, t, :], mv[:, t, 0:1], rstd[:, t:t + 1],
                                             ALU.subtract, ALU.mult)
                last.then_inc(xn_done, 1)

            for b in range(NB):
                dve.wait_ge(x_loaded[b], 16)
                for t in range(TB * b, TB * (b + 1)):
                    last = dve.bn_stats(bst[:, t, :], xt[:, t, :])
                then(last)
                for t in range(TB * b, TB * (b + 1)):
                    last = dve.bn_aggr(mv[:, t, :], bst[:, t, :])
                last.then_inc(stats_done, 1)
                if b:
                    normalise(b - 1)
            normalise(NB - 1)

            def over_e(ap):
                return ap.unsqueeze(2).broadcast_to([P, NT, E])

            dve.wait_ge(logits_ps, NB)
            dve.wait_ge(small_loaded, 16 * N_SMALL)
            dve.wait_ge(iotas_made, 1)
            then(dve.tensor_tensor(lg, ps[:, 2, 0:NT * E].rearrange("p (n e) -> p n e", e=E),
                                   brb[:].unsqueeze(1).broadcast_to([P, NT, E]), ALU.add))
            then(dve.tensor_reduce(mx1[:], lg, AX_X, ALU.max))
            then(dve.tensor_tensor(eqw, lg, over_e(mx1[:]), ALU.is_equal))
            then(dve.tensor_tensor(eqw, eqw, w8[:].unsqueeze(1).broadcast_to([P, NT, E]), ALU.mult))
            then(dve.tensor_reduce(mxw[:], eqw, AX_X, ALU.max))
            then(dve.tensor_tensor(oh, eqw, over_e(mxw[:]), ALU.is_equal))
            dve.tensor_copy(ohb[:], oh).then_inc(onehot_done, 1)
            then(dve.scalar_tensor_tensor(lg2, oh, -BIG, lg, ALU.mult, ALU.add))
            then(dve.tensor_reduce(mx2[:], lg2, AX_X, ALU.max))
            dve.tensor_tensor(dgap[:], mx2[:], mx1[:], ALU.subtract).then_inc(gap_done, 1)

            dve.wait_ge(count_ps, 1)
            pre = ps[:, 3, 0:NT * E].rearrange("p (n e) -> p e n", e=E)
            tot = ps[:, 3, NT * E:2 * NT * E].rearrange("p (n e) -> p e n", e=E)
            then(dve.tensor_copy(cnt.rearrange("p (e n) -> p e n", e=E), tot))
            then(dve.tensor_tensor_scan(csum, ones_f[:], cnt, 0.0, ALU.mult, ALU.add))
            then(dve.tensor_copy(bef[:, 1:E + 1], csum.rearrange("p (e n) -> p e n", e=E)[:, :, NT - 1]))
            then(dve.tensor_tensor(npe[:], bef[:, 1:E + 1], bef[:, 0:E], ALU.subtract))
            then(dve.tensor_scalar(npi[:], npe[:], float(P - 1), None, ALU.add))
            then(dve.tensor_single_scalar(nti[:], npi[:], P.bit_length() - 1, ALU.arith_shift_right))
            then(dve.tensor_copy(ntl[:], nti[:]))
            then(dve.tensor_tensor_scan(tinc[:], ones_f[:, 0:E], ntl[:], 0.0, ALU.mult, ALU.add))
            then(dve.tensor_tensor(tex[:], tinc[:], ntl[:], ALU.subtract))
            then(dve.scalar_tensor_tensor(dlt[:], tex[:], float(P), bef[:, 0:E], ALU.mult, ALU.subtract))
            then(dve.tensor_tensor(csum, csum, cnt, ALU.subtract))
            then(dve.tensor_tensor(rank, csum.rearrange("p (e n) -> p e n", e=E), pre, ALU.add))
            then(dve.tensor_tensor(rank, rank, dlt[:].unsqueeze(2).broadcast_to([P, E, NT]), ALU.add))
            then(dve.tensor_tensor(rank, rank, oh.rearrange("p n e -> p e n"), ALU.mult))
            then(dve.tensor_reduce(slotf[:], rank.rearrange("p e n -> p n e"), AX_X, ALU.add))
            dve.tensor_copy(slot[:], slotf[:]).then_inc(slots_done, 1)
            then(dve.tensor_tensor(cmp, jj[:].unsqueeze(2).broadcast_to([P, NST, E]),
                                   tex[:].unsqueeze(1).broadcast_to([P, NST, E]), ALU.is_ge))
            then(dve.tensor_reduce(ef[:], cmp, AX_X, ALU.add))
            then(dve.tensor_scalar(ef[:], ef[:], -1.0, None, ALU.add))
            dve.tensor_copy(eidx[:], ef[:]).then_inc(experts_known, 1)
            dve.wait_ge(gexp_done, 1)
            then(dve.tensor_scalar(gexp[:], gexp[:], 1.0, None, ALU.add))
            dve.reciprocal(gate[:], gexp[:]).then_inc(gate_done, 1)

            def copy_v(b, par):
                dve.wait_ge(v_ps, b + 1)
                dve.tensor_tensor(vt[:, par, :, :, 0:D],
                                  ps[:, MISC, :].rearrange("p (n h d) -> p n h d", n=TB, h=H),
                                  bvb[:].rearrange("p (h d) -> p h d", h=H).unsqueeze(1)
                                  .broadcast_to([P, TB, H, D]), ALU.add).then_inc(v_done, 1)

            def row_max(b, u):
                tb, h0, nh = UNITS[u]
                w = P * (tb + 1)
                two = ps[:, S_BANK[u % 2]:S_BANK[u % 2] + 2, :].rearrange("p a t -> p (a t)")
                src = two.rearrange("p (h w) -> p h w", h=nh)[:, :, 0:w]
                dve.wait_ge(s_ps, NU * b + u + 1)
                if u == 0 and not (isinstance(b, int) and b == 0):
                    dve.wait_ge(guard_ps, b)
                dve.tensor_reduce(mx[:, tb, h0:h0 + nh], src, AX_X, ALU.max).then_inc(mx_done, 1)

            def guard_out(b):
                dve.wait_ge(guard_ps, b + 1)
                if not (isinstance(b, int) and b == 0):
                    dve.wait_ge(guard_split, b)
                dve.tensor_scalar(guard[:], ps[0:H, MISC, :], -1.0, None, ALU.mult).then_inc(guard_neg, 1)

            copy_v(0, 0)
            for u in range(NU):
                row_max(0, u)
            guard_out(0)

            def tile_y(q, r):
                dve.wait_ge(ye_ps, FR * q + r + 1)
                if not first(q):
                    dve.wait_ge(ys_stored[r], 16 * q)
                dve.tensor_tensor(yst[:, r, :], ps[:, r, P:P + C], wcur[:, r, B2_AT:B2_AT + C],
                                  ALU.add).then_inc(ye_done, 1)

            sorted_tiles(dve, tile_y)

            def slot_dve(b, half, par, more, steady):
                units = [0]

                def max_upto(n):
                    while more and units[0] < min(n, NU):
                        row_max(b + 1, units[0])
                        units[0] += 1

                def norm(g):
                    src = ps[:, MISC, :].rearrange("p (n i j) -> p n i j", n=TB, i=G)
                    dve.wait_ge(yT_back, NG * b + g + 1 + Y_RING)
                    dve.reciprocal(rcp[:], src[:, :, :, D]).then_inc(rcp_done, 1)
                    dve.wait_ge(rcp_done, NG * b + g + 1)
                    if g == 0:
                        dve.wait_ge(y2_ps, b + 1)
                    dve.tensor_tensor(yn[:, :, G * D * g:G * D * (g + 1)].rearrange("p n (i d) -> p n i d", i=G),
                                      src[:, :, :, 0:D], rcp[:].unsqueeze(3).broadcast_to([P, TB, G, D]),
                                      ALU.mult).then_inc(y_norm, 1)

                for k in range(NG * TB):
                    max_upto(UNITS_BY[k])
                    if k % TB == 1 and k > TB:
                        norm(k // TB - 1)
                    if k == NG * TB - 2 and more:
                        guard_out(b + 1)
                if more:
                    copy_v(b + 1, 1 - par)
                norm(NG - 1)
                dve.wait_ge(proj_ps, ONE + b + 1)
                dve.wait_ge(base_done, ONE + b + 1)
                dve.wait_ge(out_stored[par], 16 * (half + 1))
                dve.tensor_tensor(outb[:, par], ps[:, MISC, :].rearrange("p (n c) -> p n c", n=TB),
                                  base[:, par], ALU.add).then_inc(out_done, 1)

            slots(dve, slot_dve)

        @block.gpsimd
        def _(pool):
            pool.memset(probs[:], 0.0).then_inc(zero_made, 1)
            pool.iota(w8[:], pattern=[[-1, E]], base=E, channel_multiplier=0,
                      allow_small_or_imprecise_dtypes=True)
            pool.iota(jj[:], pattern=[[1, NST]], base=0, channel_multiplier=0,
                      allow_small_or_imprecise_dtypes=True).then_inc(iotas_made, 1)

            pool.wait_ge(small_loaded, 16 * N_SMALL)
            pool.tensor_copy(wqk_dh[:].rearrange("p s (d h) -> p s d h", h=H),
                             wqkv[:, 0:2 * C].rearrange("p (s h d) -> p s d h", s=2, h=H)).then_inc(wqk_done, 1)

            def copy_x(b, par):
                pool.tensor_copy(xc[:, par, :], xnT[:, bass.ds(b * T, T)]).then_inc(xc_done, 1)

            def split_qk(b):
                pool.wait_ge(qk_copied, 2 * b + 2)
                if not (isinstance(b, int) and b == 0):
                    pool.wait_ge(parts_stored, 32 * b)
                    pool.sem_inc(pool_passed, 1)
                n = 3 * b
                pool.tensor_copy(qkp[:, :, 0, :], qkf[:]).then_inc(split_chain, 1)
                pool.wait_ge(split_chain, n + 1)
                pool.tensor_tensor(qkr[:], qkf[:], qkp[:, :, 0, :], ALU.subtract).then_inc(split_chain, 1)
                pool.wait_ge(split_chain, n + 2)
                pool.sem_inc(pool_passed, 1)
                pool.tensor_copy(qkp[:, :, 1, :], qkr[:]).then_inc(split_chain, 1)
                pool.wait_ge(split_chain, n + 3)
                pool.tensor_tensor(qkp[:, :, 2, :], qkr[:], qkp[:, :, 1, :], ALU.subtract).then_inc(qk_split, 1)

            def split_guard(b):
                pool.wait_ge(guard_neg, b + 1)
                if not (isinstance(b, int) and b == 0):
                    pool.wait_ge(guard_loaded, 16 * b)
                    pool.sem_inc(pool_passed, 1)
                n = 3 * b
                pool.tensor_copy(guard_p[:, 0, :], guard[:]).then_inc(guard_chain, 1)
                pool.wait_ge(guard_chain, n + 1)
                pool.tensor_tensor(guard_r[:], guard[:], guard_p[:, 0, :], ALU.subtract).then_inc(guard_chain, 1)
                pool.wait_ge(guard_chain, n + 2)
                pool.sem_inc(pool_passed, 1)
                pool.tensor_copy(guard_p[:, 1, :], guard_r[:]).then_inc(guard_chain, 1)
                pool.wait_ge(guard_chain, n + 3)
                pool.tensor_tensor(guard_p[:, 2, :], guard_r[:], guard_p[:, 1, :], ALU.subtract
                                   ).then_inc(guard_split, 1)

            for b in range(2):
                pool.wait_ge(xnT_done, b + 1)
                copy_x(b, b)
                split_qk(b)

            pool.wait_ge(xn_done, NB)
            pool.wait_ge(slots_done, 1)
            pool.wait_ge(zero_stored, 16)
            for t in range(NT):
                pool.indirect_dma_start(xs_dram, bass.IndirectOffsetOnAxis(ap=slot[:, t:t + 1], axis=0),
                                        xn[:, t, :], None).then_inc(scattered, 16)

            pool.wait_ge(experts_known, 1)
            pool.wait_ge(w1_loaded, 16 * 3 * E)
            pool.wait_ge(b1_done, 1)

            def tile_weights(q, r):
                n = FR * q + r
                e = pool.value_load(eidx[0:1, bass.ds(n, 1)], min_val=0, max_val=E - 1)
                if not first(q):
                    pool.wait_ge(ye_done, n - FR + 1)
                    pool.sem_inc(pool_passed, 1)
                pool.tensor_copy(wcur[:, r, :], wall[:, bass.ds(e, 1), :].rearrange("p o w -> p (o w)")
                                 ).then_inc(wcur_done, 1)

            tile_weights(0, 0)
            split_guard(0)
            for r in range(1, FR):
                tile_weights(0, r)
            with pool.Fori(1, NST // FR) as q:
                for r in range(FR):
                    tile_weights(q, r)
            for r in range(FR):
                pool.wait_ge(ys_stored[r], 16 * (NST // FR))
            pool.wait_ge(gate_done, 1)
            pool.wait_ge(small_loaded, 16 * N_SMALL)

            pool.sem_inc(base_done, ONE)

            def slot_pool(b, half, par, more, steady):
                def mask(k):
                    g, sb_ = divmod(k, TB)
                    w = T - P * sb_
                    p = probs[:, P_AT[sb_]:P_AT[sb_] + G * w].rearrange("p (h w) -> p h w", h=G)[:, :, 0:P]
                    pool.wait_ge(exp_done, ST_RING + NC_ * b + LAST_CHUNK[(g, sb_)])
                    pool.sem_inc(pool_passed, 1)
                    pool.affine_select(out=p, in_=p, compare_op=ALU.is_ge, fill=0.0, base=0,
                                       pattern=[[0, G], [1, P]], channel_multiplier=-1).then_inc(p_masked, 1)

                def gather():
                    pool.wait_ge(base_done, b + 1)
                    pool.sem_inc(pool_passed, 1)
                    pool.tensor_copy(slot_cur[:, par, :], slot[:, bass.ds(TB * b, TB)]).then_inc(idx_copied, 1)
                    pool.wait_ge(idx_copied, b + 1)
                    pool.sem_inc(pool_passed, 1)
                    for t in range(TB):
                        pool.indirect_dma_start(ysg[:, par, t, :], None, ys_dram,
                                                bass.IndirectOffsetOnAxis(ap=slot_cur[:, par, t:t + 1], axis=0)
                                                ).then_inc(gathered[par], 16)

                def residual():
                    pool.wait_ge(gathered[par], 16 * TB * (half + 1))
                    pool.wait_ge(out_done, b + 1)
                    pool.tensor_tensor(ysg[:, par], ysg[:, par],
                                       gate[:, bass.ds(TB * b, TB)].unsqueeze(2).broadcast_to([P, TB, C]),
                                       ALU.mult).then_inc(gated, 1)
                    pool.tensor_tensor(base[:, par], xt[:, bass.ds(TB * b, TB), :],
                                       bpb[:].unsqueeze(1).broadcast_to([P, TB, C]), ALU.add).then_inc(biased, 1)
                    pool.wait_ge(gated, b + 1)
                    pool.wait_ge(biased, b + 1)
                    pool.tensor_tensor(base[:, par], base[:, par], ysg[:, par], ALU.add).then_inc(base_done, 1)

                if steady:
                    pool.wait_ge(v_ps, b + 1)
                    pool.sem_inc(pool_passed, 1)
                    copy_x(b + 2, par)
                for k in range(NG * TB):
                    mask(k)
                    if k == 3 and steady:
                        split_qk(b + 2)
                    if k == 5:
                        gather()
                    if k == 9:
                        residual()
                    if k == NG * TB - 2 and more:
                        split_guard(b + 1)

            slots(pool, slot_pool)

        @block.tensor
        def _(pe):
            pe.sem_inc(pv_done, P_RING)
            pe.sem_inc(yT_back, Y_RING)
            pe.sem_inc(y2_ps, ONE)
            pe.sem_inc(proj_ps, ONE)
            pe.wait_ge(const_loaded, 16 * N_CONST)
            pe.wait_ge(small_loaded, 16 * N_SMALL)
            pe.transpose(ps[:, 3, 0:E * IC], b1r[:], ident[0:E * IC, 0:E * IC]).then_inc(b1_ps, 1)

            def logits(b):
                pe.wait_ge(xnT_done, b + 1)
                for t in range(TB * b, TB * (b + 1)):
                    last = pe.matmul(ps[:, 2, t * E:(t + 1) * E], xnT[:, t * P:(t + 1) * P], wrt[:],
                                     start=True, stop=True)
                last.then_inc(logits_ps, 1)

            for b in range(NB):
                pe.wait_ge(xn_done, b + 1)
                if b >= 2:
                    pe.wait_ge(xnT_done, b - 1)
                for t in range(TB):
                    last = pe.transpose(ps[:, b % 2, t * P:(t + 1) * P], xn[:, TB * b + t, :], ident[:])
                last.then_inc(xnT_ps, 1)
                if b:
                    logits(b - 1)
            logits(NB - 1)

            def project_qk(b, par, s):
                pe.matmul(ps[:, MISC, :], wqk_dh[:, s, :], xc[:, par, :], start=True, stop=True).then_inc(qk_ps, 1)

            def project_v(b, par):
                for t in range(TB):
                    last = pe.matmul(ps[:, MISC, t * P:(t + 1) * P], xc[:, par, t * P:(t + 1) * P],
                                     wqkv[:, 2 * C:3 * C], start=True, stop=True)
                last.then_inc(v_ps, 1)

            def score_unit(b, half, par, u):
                tb, h0, nh = UNITS[u]
                w = P * (tb + 1)
                step = 2 * T // nh
                at = 64 * par
                if tb == TB - 1 and h0 % G == 0:
                    pe.wait_ge(stack_loaded[par][h0 // G], 16 * STACK_DMAS * (half + 1))
                pe.wait_ge(mx_done, NU * b + u + 1)
                two = ps[:, S_BANK[u % 2]:S_BANK[u % 2] + 2, :].rearrange("p a t -> p (a t)")
                for n in range(nh):
                    pe.matmul(two[:, n * step:n * step + w],
                              stack[at:at + N_SCORE, 0, h0 + n, tb * P:(tb + 1) * P],
                              stack[at:at + N_SCORE, 1, h0 + n, 0:w], start=True, stop=False)
                    last = pe.matmul(two[:, n * step + w - P:n * step + w], ident_b, mask_b,
                                     start=False, stop=True)
                last.then_inc(s_ps, 1)

            def guard_back(b):
                pe.wait_ge(mx_done, S_RING + NU * (b + 1))
                for tb in range(TB):
                    last = pe.transpose(ps[0:H, MISC, tb * P:(tb + 1) * P], mx[:, tb, :], ident[:])
                last.then_inc(guard_ps, 1)

            pe.wait_ge(wqk_done, 1)
            pe.wait_ge(xc_done, 1)
            project_qk(0, 0, 0)
            pe.wait_ge(onehot_done, 1)
            pe.wait_ge(b1_done, 1)
            oh2 = ohb[:].rearrange("p n e -> p (n e)")
            pe.matmul(ps[:, 3, 0:NT * E], tri_b, oh2, start=True, stop=True)
            pe.matmul(ps[:, 3, NT * E:2 * NT * E], ones_b, oh2, start=True, stop=True).then_inc(count_ps, 1)
            pe.wait_ge(qk_copied, 1)
            project_qk(0, 0, 1)
            pe.wait_ge(xc_done, 2)
            for s in range(2):
                pe.wait_ge(qk_copied, 2 + s)
                project_qk(1, 1, s)
            pe.wait_ge(qk_copied, 4)
            project_v(0, 0)
            pe.wait_ge(slots_done, 1)
            for u in range(NU):
                score_unit(0, 0, 0, u)
            pe.wait_ge(v_done, 1)
            guard_back(0)

            def tile_transpose(q, r):
                n = FR * q + r
                pe.wait_ge(xs_loaded[r], 16 * (q + 1))
                if not first(q):
                    pe.wait_ge(ye_done, n - FR + 1)
                pe.transpose(ps[:, r, 0:P], xst[:, r, :], ident[:]).then_inc(xsT_ps, 1)

            def tile_up(q, r):
                n = FR * q + r
                pe.wait_ge(xsT_done, n + 1)
                pe.wait_ge(wcur_done, n + 1)
                if not first(q):
                    pe.wait_ge(hid_done, n - FR + 1)
                for i in range(IC):
                    last = pe.matmul(ps[:, 3 + r, i * P:(i + 1) * P],
                                     wcur[:, r, W1_AT + i * P:W1_AT + (i + 1) * P], xsT[:, r, :],
                                     start=True, stop=True)
                last.then_inc(hid_ps, 1)

            def tile_down(q, r):
                pe.wait_ge(hid_done, FR * q + r + 1)
                for i in range(IC):
                    last = pe.matmul(ps[:, r, P:P + C], hid[:, r, i, :],
                                     wcur[:, r, W2_AT + i * C:W2_AT + (i + 1) * C],
                                     start=(i == 0), stop=(i == IC - 1))
                last.then_inc(ye_ps, 1)

            def tile_step(q, r):
                if not (final(q) and r == FR - 1):
                    tile_transpose(q + 1 if r == FR - 1 else q, (r + 1) % FR)
                tile_up(q, r)
                if not (first(q) and r == 0):
                    tile_down(q - 1 if r == 0 else q, (r - 1) % FR)

            tile_transpose(0, 0)
            sorted_tiles(pe, tile_step)
            tile_down(NST // FR - 1, FR - 1)
            pe.wait_ge(ye_done, NST)
            pe.wait_ge(consts_made, 1)

            def slot_pe(b, half, par, more, steady):
                at = 64 * par
                units = [0]

                def unit_upto(n):
                    while more and units[0] < min(n, NU):
                        score_unit(b + 1, half + par, 1 - par, units[0])
                        units[0] += 1

                def chunk(n):
                    g, sb_, h0, nh = CHUNKS[n]
                    w = T - P * sb_
                    pe.wait_ge(exp_done, NC_ * b + n + 1)
                    for m in range(nh):
                        h = G * g + h0 + m
                        last = pe.matmul(ps[:, ST_BANK[n % 2], m * w:(m + 1) * w],
                                         stack[at:at + N_STACK, 1, h, P * sb_:P * (sb_ + 1)],
                                         stack[at:at + N_STACK, 0, h, P * sb_:T], start=True, stop=True)
                    last.then_inc(st_ps, 1)

                def weigh(k):
                    g, sb_ = divmod(k, TB)
                    w = T - P * sb_
                    pe.wait_ge(p_masked, NG * TB * b + k + 1)
                    if sb_ == 0:
                        pe.wait_ge(yT_copied, NG * b + g + 1)
                        if g == 0:
                            pe.wait_ge(v_done, b + 1)
                    for m in range(G):
                        last = pe.matmul(ps[32 * m:32 * m + VW, PV_BANK, P * sb_:T],
                                         vt[:, par, sb_, G * g + m, :],
                                         probs[:, P_AT[sb_] + m * w:P_AT[sb_] + (m + 1) * w],
                                         start=(sb_ == 0), stop=(sb_ == TB - 1))
                    last.then_inc(pv_done, 1)

                def y_back(g):
                    pe.wait_ge(yT_copied, ONE + NG * b + g + 1)
                    for t in range(TB):
                        last = pe.transpose(ps[:, MISC, t * P:(t + 1) * P], yTs[:, g % 2, t * P:(t + 1) * P], ident[:])
                    last.then_inc(yT_back, 1)

                pe.wait_ge(guard_loaded, 16 * (b + 1))
                n = 0
                for k in range(NG * TB):
                    while n < LAST_CHUNK[divmod(k, TB)]:
                        chunk(n)
                        n += 1
                        unit_upto(min(units[0] + 1, UNITS_BY[k]))
                    unit_upto(UNITS_BY[k])
                    if k == 1 and steady:
                        pe.wait_ge(out_done, b + 1)
                        pe.wait_ge(xc_done, b + 3)
                        project_qk(b + 2, par, 0)
                    if k == 2 and steady:
                        pe.wait_ge(qk_copied, 2 * (b + 2) + 1)
                        project_qk(b + 2, par, 1)
                    if k == TB + 1:
                        if steady:
                            pe.wait_ge(qk_copied, 2 * (b + 2) + 2)
                        else:
                            pe.wait_ge(out_done, b + 1)
                        y_back(0)
                    if k in (2 * TB + 1, 3 * TB + 1):
                        pe.wait_ge(y_norm, NG * b + k // TB - 1)
                        y_back(k // TB - 1)
                    if k == NG * TB - 2 and more:
                        pe.wait_ge(y_norm, NG * b + NG - 1)
                        guard_back(b + 1)
                    if k:
                        weigh(k - 1)
                weigh(NG * TB - 1)
                if more:
                    pe.wait_ge(guard_neg, b + 2)
                    project_v(b + 1, 1 - par)
                    pe.wait_ge(v_done, b + 2)
                else:
                    pe.wait_ge(y_norm, NG * b + NG - 1)
                y_back(NG - 1)
                pe.wait_ge(y_norm, NG * b + NG)
                for t in range(TB):
                    last = pe.transpose(ps[:, MISC, t * P:(t + 1) * P], yn[:, t, :], ident[:])
                last.then_inc(y2_ps, 1)
                pe.wait_ge(y2_copied, b + 1)
                for t in range(TB):
                    last = pe.matmul(ps[:, MISC, t * C:(t + 1) * C], yn2[:, t * P:(t + 1) * P], wpj[:],
                                     start=True, stop=True)
                last.then_inc(proj_ps, 1)

            slots(pe, slot_pe)


def top_bits(a):
    import numpy as np

    bits = np.ascontiguousarray(a, np.float32).view(np.uint32)
    kept = (bits & np.uint32(0xFFFF0000)).view(np.float32)
    return (bits >> np.uint32(16)).astype(np.uint16), (a - kept).astype(np.float32)


def shape_constants():
    import numpy as np

    pos = np.arange(T)
    slopes = (2.0 ** (-(8.0 / H) * np.arange(1, H + 1))).astype(np.float32)
    left = slopes[:, None] * pos[None, :].astype(np.float32)
    alibi = []
    for _ in range(N_ALIBI):
        part, left = top_bits(left)
        alibi.append(part)
    one = top_bits(np.ones((H, T), np.float32))[0]
    block = np.arange(CM)[:, None, None]
    before = top_bits(np.broadcast_to(np.where(pos[None, None] // 64 < block, -BIG, 0.0), (CM, H, T)).astype(np.float32))[0]
    inside = top_bits(np.broadcast_to(pos[None, None] // 64 == block, (CM, H, T)).astype(np.float32))[0]
    stack_q = np.concatenate([np.stack([one] * N_ALIBI), before])
    stack_k = np.concatenate([np.stack(alibi), inside, np.stack([one] * 3)])
    r = np.arange(P)
    bf = np.stack([np.eye(P), np.where(r[None] > r[:, None], -BIG, 0.0), r[:, None] < r[None], np.ones((P, P))], 1)
    return {"c_ident": np.eye(P, dtype=np.float32), "c_bf": top_bits(bf.astype(np.float32))[0],
            "c_stack_q": stack_q, "c_stack_k": stack_k}


_INS = ["L0_attn_x", "L0_attn_w_attn", "L0_attn_b_attn", "L0_attn_w_proj", "L0_attn_b_proj", "L0_ffn_w1",
        "L0_ffn_b1", "L0_ffn_w2", "L0_ffn_b2", "L0_ffn_wr", "L0_ffn_br"]


def kernel(**inputs):
    import numpy as np
    import concourse.bacc as bacc
    from concourse.bass_utils import run_bass_kernel_spmd

    nc = bacc.Bacc("TRN2", target_bir_lowering=False, num_devices=1)
    arrays = {name: np.ascontiguousarray(inputs[name]) for name in _INS}
    arrays.update(shape_constants())
    args = [nc.dram_tensor(name, a.shape, mybir.dt.from_np(a.dtype), kind="ExternalInput").ap()
            for name, a in arrays.items()]
    out = nc.dram_tensor("out", (NB, T, C), F32, kind="ExternalOutput").ap()
    block_kernel(nc, *args, out)
    return run_bass_kernel_spmd(nc, [arrays], core_ids=[0]).results[0]["out"]
```

```python
from contextlib import ExitStack

import concourse.bass as bass
from concourse import mybir

F32 = mybir.dt.float32
BF16 = mybir.dt.bfloat16
U16 = mybir.dt.uint16
U32 = mybir.dt.uint32
I32 = mybir.dt.int32
ALU = mybir.AluOpType
ACT = mybir.ActivationFunctionType
AX_X = mybir.AxisListType.X

P = 128
NB = 8
T = 512
C = 128
H = 16
D = C // H
TB = T // P
NT = NB * TB
E = 8
I = 512
IC = I // P
NST = NT + E - 1
EPS = 1e-5
BIG = 1e30
Q_SCALE = float(D) ** -0.5

W1_AT, B1_AT, W2_AT, B2_AT = 0, I, I + IC, I + IC + IC * C
WCOLS = B2_AT + C
FR = 3

PARTS_Q = (0, 0, 0, 1, 1, 2)
PARTS_K = (0, 1, 2, 0, 1, 0)
N_PROD = len(PARTS_Q) * D
N_ALIBI = 3
CM = T // 64
N_SCORE = N_PROD + N_ALIBI + CM
N_STACK = N_SCORE + 3

G = 4
NG = H // G
VW = D + 1


def score_chunks():
    out = []
    for g in range(NG):
        for sb in range(TB):
            nh = {0: 1, 1: 1, 2: 2, 3: 4}[sb]
            out += [(g, sb, h0, nh) for h0 in range(0, G, nh)]
    return out


def max_units():
    return [(3, 0, 2), (3, 2, 2), (2, 0, 2), (2, 2, 2), (1, 0, 4), (0, 0, 4)]


CHUNKS = score_chunks()
UNITS = max_units()
STEPS = len(CHUNKS)
GSTEPS = STEPS // NG
TAIL = 8
SPAN = STEPS + TAIL
NU = len(UNITS)
ENDS = {}
for _n, (_g, _sb, _h, _nh) in enumerate(CHUNKS):
    ENDS[TB * _g + _sb] = _n + 1

UNIT_AT = {0: 0, 2: 1, 3: 2, 5: 3, 6: 4, 8: 5}
LEAD = 3
GUARD_AT = {GSTEPS - 1: 1, 3 * GSTEPS - 1: 2}
V_AT, Q_AT, K_AT = 18, 21, 28
XC_AT, SPLIT_AT, PARTS_AT = 12, K_AT + 2, K_AT + 6
GATHER_AT, RESIDUAL_AT = 14, 24
Y2_AT, PROJ_AT = SPAN - 3, SPAN - 1


def weigh_at(k):
    return ENDS[k] + 1


def y_back_at(g):
    return weigh_at(TB * g + TB - 1) + 2


P_AT = [G * sum(T - P * n for n in range(sb_)) for sb_ in range(TB)]
P_COLS = P_AT[-1] + G * P

STACK_DMAS = 7

ST_RING, P_RING, S_RING, Y_RING = 2, TB, 2, 2
ONE = 1


def block_kernel(nc, x, w_attn, b_attn, w_proj, b_proj, w1, b1, w2, b2, wr, br,
                 c_ident, c_bf, c_stack_q, c_stack_k, out):
    with ExitStack() as ctx:
        def sb(name, shape, dt=F32):
            return ctx.enter_context(nc.sbuf_tensor(name, shape, dt))

        def sem(name):
            return ctx.enter_context(nc.semaphore(name))

        xs_dram = nc.dram_tensor("xs_sorted", (NST * P, C), F32, kind="Internal").ap()
        ys_dram = nc.dram_tensor("ys_sorted", (NST * P, C), F32, kind="Internal").ap()
        parts_dram = nc.dram_tensor("qk_parts", (2, 2, 3, D, H, T), BF16, kind="Internal").ap()
        guard_dram = nc.dram_tensor("guard_parts", (2, 3, H // 2, T), BF16, kind="Internal").ap()

        xt = sb("xt", [P, NT, C])
        xn = sb("xn", [P, NT, C])
        xnT = sb("xnT", [P, NT * P])
        wall = sb("wall", [P, E, WCOLS])
        wcur = sb("wcur", [P, FR, WCOLS])
        stack = sb("stack", [P, 2, H, T], BF16)
        probs = sb("probs", [P, P_COLS])
        vt = sb("vt", [P, 2, TB, H, VW])
        xc = sb("xc", [P, 2, T])
        qkf = sb("qkf", [P, 2, T])
        qkr = sb("qkr", [P, 2, T])
        qkp = sb("qkp", [P, 2, 3, T], BF16)
        yn = sb("yn", [P, TB, C])
        yn2 = sb("yn2", [P, T])
        rcp = sb("rcp", [P, TB, G])
        mx = sb("mx", [P, TB, H])
        guard_r = sb("guard_r", [H // 2, T])
        guard_p = sb("guard_p", [H // 2, 3, T], BF16)
        reuse = xn[:].rearrange("p (b q n) c -> p b q n c", b=4, q=2)
        ysg, base, outb, yTq = (reuse[:, n] for n in range(4))
        yTs = yTq.rearrange("p q n c -> p q (n c)")
        slot_cur = sb("slot_cur", [P, 2, TB], U32)
        xst = sb("xst", [P, FR, C])
        xsT = sb("xsT", [P, FR, P])
        hid = sb("hid", [P, FR, IC, P])
        yst = sb("yst", [P, FR, C])
        wqkv = sb("wqkv", [P, 3 * C])
        wqk_dh = sb("wqk_dh", [P, 2, C])
        wpj = sb("wpj", [P, C])
        wrt = sb("wrt", [P, E])
        bqk = sb("bqk", [P, 2])
        bqk_s = sb("bqk_s", [P, 2])
        bvb = sb("bvb", [P, C])
        bpb = sb("bpb", [P, C])
        brb = sb("brb", [P, E])
        b1r = sb("b1r", [E * IC, P])
        ident = sb("ident", [P, P])
        cbf = sb("cbf", [P, 4, P], BF16)
        ident_b, mask_b, tri_b, ones_b = (cbf[:, n, :] for n in range(4))
        bst = sb("bst", [P, NT, 6])
        mv = sb("mv", [P, NT, 2])
        std = sb("std", [P, NT])
        rstd = sb("rstd", [P, NT])
        eps = sb("eps", [P, 1])
        tmp = wcur[:].rearrange("p r w -> p (r w)")
        lg, lg2, eqw, oh = (tmp[:, n * NT * E:(n + 1) * NT * E].rearrange("p (n e) -> p n e", e=E) for n in range(4))
        cnt, csum, rank_f = (tmp[:, n * NT * E:(n + 1) * NT * E] for n in range(4, 7))
        rank = rank_f.rearrange("p (e n) -> p e n", e=E)
        cmp = tmp[:, 7 * NT * E:7 * NT * E + NST * E].rearrange("p (j e) -> p j e", e=E)
        ohb = sb("ohb", [P, NT, E], BF16)
        w8 = sb("w8", [P, E])
        mx1 = sb("mx1", [P, NT])
        mxw = sb("mxw", [P, NT])
        mx2 = sb("mx2", [P, NT])
        dgap = sb("dgap", [P, NT])
        gexp = sb("gexp", [P, NT])
        gate = sb("gate", [P, NT])
        ones_f = sb("ones_f", [P, E * NT])
        bef = sb("bef", [P, E + 1])
        npe = sb("npe", [P, E])
        npi = sb("npi", [P, E], I32)
        nti = sb("nti", [P, E], I32)
        ntl = sb("ntl", [P, E])
        tinc = sb("tinc", [P, E])
        tex = sb("tex", [P, E])
        dlt = sb("dlt", [P, E])
        slotf = sb("slotf", [P, NT])
        slot = sb("slot", [P, NT], U32)
        jj = sb("jj", [P, NST])
        ef = sb("ef", [P, NST])
        eidx = sb("eidx", [P, NST], I32)

        ps = ctx.enter_context(nc.psum_tensor("ps", [P, 8, T], F32))
        S_BANK = (0, 2)
        ST_BANK = (4, 5)
        PV_BANK, MISC = 6, 7
        QK_BANK = (4, 5)

        x_loaded = [sem(f"x_loaded{b}") for b in range(NB)]
        small_loaded = sem("small_loaded")
        const_loaded = sem("const_loaded")
        proj_loaded = sem("proj_loaded")
        rows_loaded = sem("rows_loaded")
        w1_loaded = sem("w1_loaded")
        zero_made = sem("zero_made")
        zero_stored = sem("zero_stored")
        consts_made = sem("consts_made")
        iotas_made = sem("iotas_made")
        dve_chain = sem("dve_chain")
        stats_done = sem("stats_done")
        std_done = sem("std_done")
        xn_done = sem("xn_done")
        xnT_ps = sem("xnT_ps")
        xnT_done = sem("xnT_done")
        b1_ps = sem("b1_ps")
        b1_done = sem("b1_done")
        logits_ps = sem("logits_ps")
        onehot_done = sem("onehot_done")
        count_ps = sem("count_ps")
        gap_done = sem("gap_done")
        gexp_done = sem("gexp_done")
        gate_done = sem("gate_done")
        slots_done = sem("slots_done")
        experts_known = sem("experts_known")
        scattered = sem("scattered")
        bias_scaled = sem("bias_scaled")
        xs_loaded = [sem(f"xs_loaded{r}") for r in range(FR)]
        wcur_done = sem("wcur_done")
        xsT_ps = sem("xsT_ps")
        xsT_done = sem("xsT_done")
        hid_ps = sem("hid_ps")
        hid_done = sem("hid_done")
        ye_ps = sem("ye_ps")
        ye_done = sem("ye_done")
        ys_stored = [sem(f"ys_stored{r}") for r in range(FR)]
        wqk_done = sem("wqk_done")
        xc_done = sem("xc_done")
        qk_ps = sem("qk_ps")
        qk_copied = sem("qk_copied")
        qk_left = sem("qk_left")
        qk_middle = sem("qk_middle")
        qk_split = sem("qk_split")
        parts_stored = sem("parts_stored")
        stack_loaded = [sem(f"stack_loaded{p}") for p in range(2)]
        v_ps = sem("v_ps")
        v_done = sem("v_done")
        s_ps = sem("s_ps")
        mx_done = sem("mx_done")
        guard_ps = sem("guard_ps")
        guard_first = sem("guard_first")
        guard_left = sem("guard_left")
        guard_middle = sem("guard_middle")
        guard_split = sem("guard_split")
        passed, passed_pool = sem("passed"), sem("passed_pool")
        guard_stored = sem("guard_stored")
        guard_loaded = sem("guard_loaded")
        st_ps = sem("st_ps")
        exp_done = sem("exp_done")
        p_masked = sem("p_masked")
        pv_done = sem("pv_done")
        yT_copied = sem("yT_copied")
        yT_back = sem("yT_back")
        rcp_done = sem("rcp_done")
        y_norm = sem("y_norm")
        y2_ps = sem("y2_ps")
        y2_copied = sem("y2_copied")
        proj_ps = sem("proj_ps")
        idx_copied = sem("idx_copied")
        gathered = [sem(f"gathered{p}") for p in range(2)]
        gated = sem("gated")
        biased = sem("biased")
        base_done = sem("base_done")
        out_done = sem("out_done")
        out_stored = [sem(f"out_stored{p}") for p in range(2)]

        N_SMALL, N_CONST, N_PROJ, N_ROWS = 7, 2, 2, 4

        def timeline(eng, at):
            def window(b, half, par, following):
                for pos in range(TAIL, SPAN):
                    at(b, half, par, pos)
                    if pos >= STEPS and following:
                        at(b + 1, half + par, 1 - par, pos - STEPS)

            for pos in range(TAIL):
                at(0, 0, 0, pos)
            with eng.Fori(0, (NB - 2) // 2) as i:
                for par in range(2):
                    window(2 * i + par, i, par, True)
            for b in (NB - 2, NB - 1):
                window(b, b // 2, b % 2, b + 1 < NB)

        def has(b):
            return not isinstance(b, int) or b < NB

        def max_group(b, half, par, pos):
            if pos >= STEPS or pos % GSTEPS not in UNIT_AT:
                return None
            g = pos // GSTEPS + LEAD
            if g >= NG:
                b, half, par, g = b + 1, half + par, 1 - par, g - NG
            return (b, half, par, g, UNIT_AT[pos % GSTEPS]) if has(b) else None

        def guard_pair(b, half, par, pos):
            if pos not in GUARD_AT:
                return None
            if GUARD_AT[pos] == 1:
                return b, half, par, 1
            return (b + 1, half + par, 1 - par, 0) if has(b + 1) else None

        def sorted_tiles(eng, body):
            for r in range(FR):
                body(0, r)
            with eng.Fori(1, NST // FR - 1) as q:
                for r in range(FR):
                    body(q, r)
            for r in range(FR):
                body(NST // FR - 1, r)

        def first(q):
            return isinstance(q, int) and q == 0

        def final(q):
            return isinstance(q, int) and q == NST // FR - 1

        block = ctx.enter_context(nc.Block())

        @block.sync
        def _(sp):
            for par in range(2):
                sp.sem_inc(out_stored[par], 16 * ONE)
            for b in range(NB):
                sp.dma_start(xt[:, TB * b:TB * (b + 1), :],
                             x[b].rearrange("(n p) c -> p n c", p=P)).then_inc(x_loaded[b], 16)
            sp.dma_start(bvb[:], b_attn[2 * C:3 * C].partition_broadcast(P)).then_inc(small_loaded, 16)
            sp.dma_start(bpb[:], b_proj.partition_broadcast(P)).then_inc(small_loaded, 16)
            sp.dma_start(brb[:], br.partition_broadcast(P)).then_inc(small_loaded, 16)
            sp.dma_start(b1r[:], b1.rearrange("e (i p) -> (e i) p", p=P)).then_inc(small_loaded, 16)
            sp.dma_start(wpj[:], w_proj).then_inc(small_loaded, 16)
            for par in range(2):
                at = 64 * par
                sp.dma_start(stack[at + N_PROD:at + N_SCORE, 0].bitcast(U16), c_stack_q).then_inc(rows_loaded, 16)
                sp.dma_start(stack[at + N_PROD:at + N_STACK, 1].bitcast(U16), c_stack_k).then_inc(rows_loaded, 16)
            sp.wait_ge(zero_made, 1)
            zeros = probs[:, 0:NST * C]
            sp.dma_start(xs_dram.rearrange("(p n) c -> p (n c)", p=P), zeros).then_inc(zero_stored, 16)

            for e in range(E):
                sp.dma_start(wall[:, e, W1_AT:W1_AT + I], w1[e]).then_inc(w1_loaded, 16)
                sp.dma_start(wall[:, e, W2_AT:W2_AT + IC * C].rearrange("p (i c) -> p i c", i=IC),
                             w2[e].rearrange("(i p) c -> p i c", p=P)).then_inc(w1_loaded, 16)
                sp.dma_start(wall[:, e, B2_AT:B2_AT + C], b2[e].partition_broadcast(P)).then_inc(w1_loaded, 16)

            def store_parts(b, par):
                sp.wait_ge(qk_split, b + 1)
                for s in range(2):
                    sp.dma_start(parts_dram[par, s].rearrange("j d h t -> (d h) j t"),
                                 qkp[:, s]).then_inc(parts_stored, 16)
                sp.wait_ge(parts_stored, 32 * b + 32)

            def load_stack(par):
                at = 64 * par

                def one(s, row, first_part, n_parts):
                    dst = stack[at + D * row:at + D * (row + n_parts), s]
                    src = parts_dram[par, s, first_part:first_part + n_parts]
                    sp.dma_start(dst, src.rearrange("j d h t -> (j d) h t")).then_inc(stack_loaded[par], 16)

                for s, parts in ((0, PARTS_Q), (1, PARTS_K)):
                    row = 0
                    while row < len(parts):
                        n = 1
                        while row + n < len(parts) and parts[row + n] == parts[row] + n:
                            n += 1
                        one(s, row, parts[row], n)
                        row += n

            def load_guard(b, par, pair):
                n = 2 * b + pair + 1
                sp.wait_ge(guard_split, n)
                sp.dma_start(guard_dram[pair].rearrange("j h t -> h j t"), guard_p[:]).then_inc(guard_stored, 16)
                sp.wait_ge(guard_stored, 16 * n)
                row = 64 * par + N_SCORE
                sp.dma_start(stack[row:row + 3, 0, pair * H // 2:(pair + 1) * H // 2, :], guard_dram[pair]
                             ).then_inc(guard_loaded, 16)

            for b in range(2):
                store_parts(b, b)
                if b == 0:
                    sp.wait_ge(rows_loaded, 16 * N_ROWS)
                load_stack(b)
            load_guard(0, 0, 0)
            sp.wait_ge(scattered, 16 * NT)

            def load_tile(q, r):
                if not first(q):
                    sp.wait_ge(xsT_ps, FR * (q - 1) + r + 1)
                sp.dma_start(xst[:, r, :], xs_dram[bass.ds((FR * q + r) * P, P), :]).then_inc(xs_loaded[r], 16)

            sorted_tiles(sp, load_tile)

            def io_at(b, half, par, pos):
                pair = guard_pair(b, half, par, pos)
                if pair:
                    load_guard(pair[0], pair[2], pair[3])
                if pos == PARTS_AT and has(b + 2):
                    store_parts(b + 2, par)
                if pos == STEPS and has(b + 2):
                    sp.wait_ge(st_ps, STEPS * b + STEPS)
                    load_stack(par)
                if pos == PROJ_AT:
                    sp.wait_ge(out_done, ONE + b + 1)
                    dst = out[bass.ds(b, 1), :, :].rearrange("o (n p) c -> p (o n) c", p=P)
                    sp.dma_start(dst, outb[:, par]).then_inc(out_stored[par], 16)

            timeline(sp, io_at)
            for par in range(2):
                sp.wait_ge(out_stored[par], 16 * (ONE + NB // 2))

        @block.scalar
        def _(act):
            act.dma_start(ident[:], c_ident).then_inc(const_loaded, 16)
            act.dma_start(cbf[:].bitcast(U16), c_bf).then_inc(const_loaded, 16)
            act.dma_start(wqkv[:], w_attn).then_inc(proj_loaded, 16)
            act.dma_start(wrt[:], wr).then_inc(proj_loaded, 16)
            for s in range(2):
                act.dma_start(bqk[:, s:s + 1], b_attn[s * C:(s + 1) * C].rearrange("(h d o) -> d h o", d=D, o=1),
                              allow_slow_non_contiguous=True).then_inc(small_loaded, 16)
            act.sem_inc(exp_done, ST_RING)
            act.sem_inc(yT_copied, ONE)

            def copy_qk(b, s, bank=MISC):
                if s == 0 and not (isinstance(b, int) and b == 0):
                    act.wait_ge(qk_split, b)
                    act.wait_ge(parts_stored, 32 * b)
                act.wait_ge(qk_ps, 2 * b + s + 1)
                scale = Q_SCALE if s == 0 else 1.0
                act.activation(qkf[:, s, :], ps[:, bank, :], ACT.Identity, bias=bqk_s[:, s:s + 1], scale=scale)
                act.activation(qkp[:, s, 0, :], ps[:, bank, :], ACT.Identity, bias=bqk_s[:, s:s + 1], scale=scale
                               ).then_inc(qk_copied, 1)

            def middle_qk(b):
                act.wait_ge(qk_left, b + 1)
                act.copy(qkp[:, :, 1, :], qkr[:]).then_inc(qk_middle, 1)

            def guard_high(n):
                act.wait_ge(guard_ps, n + 1)
                if not (isinstance(n, int) and n == 0):
                    act.wait_ge(guard_loaded, 16 * n)
                act.mul(guard_p[:, 0, :], ps[0:H // 2, MISC, :], -1.0).then_inc(guard_first, 1)

            def guard_mid(n):
                act.wait_ge(guard_left, n + 1)
                act.copy(guard_p[:, 1, :], guard_r[:]).then_inc(guard_middle, 1)

            for b in range(NB + 2):
                if b < NB:
                    act.wait_ge(stats_done, b + 1)
                    act.activation(std[:, TB * b:TB * (b + 1)], mv[:, TB * b:TB * (b + 1), 1], ACT.Sqrt,
                                   bias=eps[:]).then_inc(std_done, 1)
                b -= 2
                if b < 0:
                    continue
                if b == 4:
                    act.wait_ge(small_loaded, 16 * N_SMALL)
                    act.mul(bqk_s[:, 0:1], bqk[:, 0:1], Q_SCALE).then_inc(bias_scaled, 1)
                    act.copy(bqk_s[:, 1:2], bqk[:, 1:2]).then_inc(bias_scaled, 1)
                    act.wait_ge(bias_scaled, 2)
                    for s in range(2):
                        copy_qk(0, s, QK_BANK[s])
                act.wait_ge(xnT_ps, b + 1)
                act.copy(xnT[:, b * T:(b + 1) * T], ps[:, b % 2, :]).then_inc(xnT_done, 1)
            middle_qk(0)
            act.wait_ge(b1_ps, 1)
            act.copy(wall[:, :, B1_AT:B1_AT + IC], ps[:, 3, 0:E * IC].rearrange("p (e i) -> p e i", e=E)
                     ).then_inc(b1_done, 1)
            for s in range(2):
                copy_qk(1, s, QK_BANK[s])
            act.wait_ge(gap_done, 1)
            act.activation(gexp[:], dgap[:], ACT.Exp).then_inc(gexp_done, 1)
            middle_qk(1)
            guard_high(0)
            guard_mid(0)

            def tile_act(q, r):
                n = FR * q + r
                act.wait_ge(xsT_ps, n + 1)
                if not first(q):
                    act.wait_ge(hid_ps, n - FR + 1)
                act.copy(xsT[:, r, :], ps[:, r, 0:P]).then_inc(xsT_done, 1)

            def tile_gelu(q, r):
                n = FR * q + r
                act.wait_ge(hid_ps, n + 1)
                if not first(q):
                    act.wait_ge(ye_ps, n - FR + 1)
                for i in range(IC):
                    act.activation(hid[:, r, i, :], ps[:, 3 + r, i * P:(i + 1) * P], ACT.Gelu,
                                   bias=wcur[:, r, B1_AT + i:B1_AT + i + 1]).then_inc(hid_done, 1)

            def tile_pair(q, r):
                if not (final(q) and r == FR - 1):
                    tile_act(q + 1 if r == FR - 1 else q, (r + 1) % FR)
                tile_gelu(q, r)

            tile_act(0, 0)
            sorted_tiles(act, tile_pair)

            act.wait_ge(zero_stored, 16)

            def act_at(b, half, par, pos):
                if pos < STEPS:
                    g, sb_, h0, nh = CHUNKS[pos]
                    w = T - P * sb_
                    if h0 == 0:
                        act.wait_ge(pv_done, NG * TB * b + TB * g + sb_ + 1)
                    act.wait_ge(st_ps, STEPS * b + pos + 1)
                    at = P_AT[sb_] + h0 * w
                    act.activation(probs[:, at:at + nh * w].rearrange("p (h w) -> p h w", h=nh),
                                   ps[:, ST_BANK[pos % 2], 0:nh * w].rearrange("p (h w) -> p h w", h=nh),
                                   ACT.Exp).then_inc(exp_done, 1)
                for g in range(NG):
                    if pos == weigh_at(TB * g + TB - 1):
                        act.wait_ge(pv_done, P_RING + NG * TB * b + TB * g + TB)
                        act.wait_ge(yT_back, NG * b + g + 1)
                        act.copy(yTs[:, g % 2, :], ps[:, PV_BANK, :]).then_inc(yT_copied, 1)
                for s, at in enumerate((Q_AT, K_AT)):
                    if pos == at + 1 and has(b + 2):
                        copy_qk(b + 2, s)
                if pos == SPLIT_AT and has(b + 2):
                    middle_qk(b + 2)
                pair = guard_pair(b, half, par, pos)
                if pair:
                    guard_high(2 * pair[0] + pair[3])
                pair = guard_pair(b, half, par, pos - 1)
                if pair:
                    guard_mid(2 * pair[0] + pair[3])
                if pos == Y2_AT:
                    act.wait_ge(proj_ps, b + 1)
                    act.wait_ge(y2_ps, ONE + b + 1)
                    act.copy(yn2[:], ps[:, MISC, :]).then_inc(y2_copied, 1)

            timeline(act, act_at)

        @block.vector
        def _(dve):
            chain = [0]

            def then(ins):
                chain[0] += 1
                ins.then_inc(dve_chain, 1)
                dve.wait_ge(dve_chain, chain[0])

            dve.memset(ones_f[:], 1.0)
            dve.memset(bef[:, 0:1], 0.0)
            dve.memset(eps[:], EPS)
            dve.memset(ps[:, PV_BANK, :], 0.0)
            dve.memset(vt[:], 1.0).then_inc(consts_made, 1)
            dve.sem_inc(mx_done, S_RING)
            dve.sem_inc(out_done, ONE)

            def normalise(b):
                dve.wait_ge(std_done, b + 1)
                then(dve.reciprocal(rstd[:, TB * b:TB * (b + 1)], std[:, TB * b:TB * (b + 1)]))
                for t in range(TB * b, TB * (b + 1)):
                    last = dve.tensor_scalar(xn[:, t, :], xt[:, t, :], mv[:, t, 0:1], rstd[:, t:t + 1],
                                             ALU.subtract, ALU.mult)
                last.then_inc(xn_done, 1)

            for b in range(NB):
                dve.wait_ge(x_loaded[b], 16)
                for t in range(TB * b, TB * (b + 1)):
                    last = dve.bn_stats(bst[:, t, :], xt[:, t, :])
                then(last)
                for t in range(TB * b, TB * (b + 1)):
                    last = dve.bn_aggr(mv[:, t, :], bst[:, t, :])
                last.then_inc(stats_done, 1)
                if b:
                    normalise(b - 1)
            normalise(NB - 1)

            def split_qk(b):
                dve.wait_ge(qk_copied, 2 * b + 2)
                dve.tensor_tensor(qkr[:], qkf[:], qkp[:, :, 0, :], ALU.subtract).then_inc(qk_left, 1)

            def last_qk(b):
                dve.wait_ge(qk_middle, b + 1)
                dve.tensor_tensor(qkp[:, :, 2, :], qkr[:], qkp[:, :, 1, :], ALU.subtract).then_inc(qk_split, 1)

            split_qk(0)
            last_qk(0)

            def over_e(ap):
                return ap.unsqueeze(2).broadcast_to([P, NT, E])

            dve.wait_ge(logits_ps, NB)
            dve.wait_ge(small_loaded, 16 * N_SMALL)
            dve.wait_ge(iotas_made, 1)
            then(dve.tensor_tensor(lg, ps[:, 2, 0:NT * E].rearrange("p (n e) -> p n e", e=E),
                                   brb[:].unsqueeze(1).broadcast_to([P, NT, E]), ALU.add))
            then(dve.tensor_reduce(mx1[:], lg, AX_X, ALU.max))
            then(dve.tensor_tensor(eqw, lg, over_e(mx1[:]), ALU.is_equal))
            then(dve.tensor_tensor(eqw, eqw, w8[:].unsqueeze(1).broadcast_to([P, NT, E]), ALU.mult))
            then(dve.tensor_reduce(mxw[:], eqw, AX_X, ALU.max))
            then(dve.tensor_tensor(oh, eqw, over_e(mxw[:]), ALU.is_equal))
            dve.tensor_copy(ohb[:], oh).then_inc(onehot_done, 1)
            then(dve.scalar_tensor_tensor(lg2, oh, -BIG, lg, ALU.mult, ALU.add))
            then(dve.tensor_reduce(mx2[:], lg2, AX_X, ALU.max))
            dve.tensor_tensor(dgap[:], mx2[:], mx1[:], ALU.subtract).then_inc(gap_done, 1)

            dve.wait_ge(count_ps, 1)
            pre = ps[:, 3, 0:NT * E].rearrange("p (n e) -> p e n", e=E)
            tot = ps[:, 3, NT * E:2 * NT * E].rearrange("p (n e) -> p e n", e=E)
            then(dve.tensor_copy(cnt.rearrange("p (e n) -> p e n", e=E), tot))
            then(dve.tensor_tensor_scan(csum, ones_f[:], cnt, 0.0, ALU.mult, ALU.add))
            then(dve.tensor_copy(bef[:, 1:E + 1], csum.rearrange("p (e n) -> p e n", e=E)[:, :, NT - 1]))
            then(dve.tensor_tensor(npe[:], bef[:, 1:E + 1], bef[:, 0:E], ALU.subtract))
            then(dve.tensor_scalar(npi[:], npe[:], float(P - 1), None, ALU.add))
            then(dve.tensor_single_scalar(nti[:], npi[:], P.bit_length() - 1, ALU.arith_shift_right))
            then(dve.tensor_copy(ntl[:], nti[:]))
            then(dve.tensor_tensor_scan(tinc[:], ones_f[:, 0:E], ntl[:], 0.0, ALU.mult, ALU.add))
            then(dve.tensor_tensor(tex[:], tinc[:], ntl[:], ALU.subtract))
            then(dve.scalar_tensor_tensor(dlt[:], tex[:], float(P), bef[:, 0:E], ALU.mult, ALU.subtract))
            then(dve.tensor_tensor(csum, csum, cnt, ALU.subtract))
            then(dve.tensor_tensor(rank, csum.rearrange("p (e n) -> p e n", e=E), pre, ALU.add))
            then(dve.tensor_tensor(rank, rank, dlt[:].unsqueeze(2).broadcast_to([P, E, NT]), ALU.add))
            then(dve.tensor_tensor(rank, rank, oh.rearrange("p n e -> p e n"), ALU.mult))
            then(dve.tensor_reduce(slotf[:], rank.rearrange("p e n -> p n e"), AX_X, ALU.add))
            dve.tensor_copy(slot[:], slotf[:]).then_inc(slots_done, 1)
            then(dve.tensor_tensor(cmp, jj[:].unsqueeze(2).broadcast_to([P, NST, E]),
                                   tex[:].unsqueeze(1).broadcast_to([P, NST, E]), ALU.is_ge))
            then(dve.tensor_reduce(ef[:], cmp, AX_X, ALU.add))
            then(dve.tensor_scalar(ef[:], ef[:], -1.0, None, ALU.add))
            dve.tensor_copy(eidx[:], ef[:]).then_inc(experts_known, 1)
            dve.wait_ge(gexp_done, 1)
            then(dve.tensor_scalar(gexp[:], gexp[:], 1.0, None, ALU.add))
            dve.reciprocal(gate[:], gexp[:]).then_inc(gate_done, 1)
            split_qk(1)
            last_qk(1)

            def copy_v(b, par):
                dve.wait_ge(v_ps, b + 1)
                dve.tensor_tensor(vt[:, par, :, :, 0:D],
                                  ps[:, MISC, :].rearrange("p (n h d) -> p n h d", n=TB, h=H),
                                  bvb[:].rearrange("p (h d) -> p h d", h=H).unsqueeze(1)
                                  .broadcast_to([P, TB, H, D]), ALU.add).then_inc(v_done, 1)

            def row_max(b, g, u):
                tb, h0, nh = UNITS[u]
                w = P * (tb + 1)
                two = ps[:, S_BANK[u % 2]:S_BANK[u % 2] + 2, :].rearrange("p a t -> p (a t)")
                src = two.rearrange("p (h w) -> p h w", h=nh)[:, :, 0:w]
                dve.wait_ge(s_ps, NU * (NG * b + g) + u + 1)
                if u == 0 and g % 2 == 0 and not (isinstance(b, int) and b == 0):
                    dve.wait_ge(guard_ps, 2 * b - 1 + g // 2)
                dve.tensor_reduce(mx[:, tb, G * g + h0:G * g + h0 + nh], src, AX_X, ALU.max).then_inc(mx_done, 1)

            def guard_rest(n):
                dve.wait_ge(guard_first, n + 1)
                dve.scalar_tensor_tensor(guard_r[:], ps[0:H // 2, MISC, :], -1.0, guard_p[:, 0, :],
                                         ALU.mult, ALU.subtract).then_inc(guard_left, 1)

            def guard_last(n):
                dve.wait_ge(guard_middle, n + 1)
                dve.tensor_tensor(guard_p[:, 2, :], guard_r[:], guard_p[:, 1, :], ALU.subtract
                                  ).then_inc(guard_split, 1)

            copy_v(0, 0)
            for g in range(LEAD):
                for u in range(NU):
                    row_max(0, g, u)
                if g == 1:
                    guard_rest(0)
                    guard_last(0)

            def expert_weights(q, r):
                e = dve.value_load(eidx[0:1, bass.ds(FR * q + r, 1)], min_val=0, max_val=E - 1)
                dve.tensor_copy(wcur[:, r, :], wall[:, bass.ds(e, 1), :].rearrange("p o w -> p (o w)")
                                ).then_inc(wcur_done, 1)

            dve.wait_ge(w1_loaded, 16 * 3 * E)
            dve.wait_ge(b1_done, 1)
            dve.wait_ge(experts_known, 1)
            for r in range(FR):
                expert_weights(0, r)

            def tile_y(q, r):
                dve.wait_ge(ye_ps, FR * q + r + 1)
                if not first(q):
                    dve.wait_ge(ys_stored[r], 16 * q)
                dve.tensor_tensor(yst[:, r, :], ps[:, r, P:P + C], wcur[:, r, B2_AT:B2_AT + C],
                                  ALU.add).then_inc(ye_done, 1)
                if not final(q):
                    dve.wait_ge(ye_done, FR * q + r + 1)
                    dve.sem_inc(passed, 1)
                    expert_weights(q + 1, r)

            sorted_tiles(dve, tile_y)

            def dve_at(b, half, par, pos):
                unit = max_group(b, half, par, pos)
                if unit:
                    row_max(unit[0], unit[3], unit[4])
                pair = guard_pair(b, half, par, pos)
                if pair:
                    guard_rest(2 * pair[0] + pair[3])
                pair = guard_pair(b, half, par, pos - 1)
                if pair:
                    guard_last(2 * pair[0] + pair[3])
                if pos == SPLIT_AT and has(b + 2):
                    split_qk(b + 2)
                if pos == SPLIT_AT + 1 and has(b + 2):
                    last_qk(b + 2)
                if pos == V_AT and has(b + 1):
                    copy_v(b + 1, 1 - par)
                for g in range(NG):
                    if pos != y_back_at(g):
                        continue
                    src = ps[:, MISC, :].rearrange("p (n i j) -> p n i j", n=TB, i=G)
                    dve.wait_ge(yT_back, NG * b + g + 1 + Y_RING)
                    dve.reciprocal(rcp[:], src[:, :, :, D]).then_inc(rcp_done, 1)
                    dve.wait_ge(rcp_done, NG * b + g + 1)
                    if g == 0:
                        dve.wait_ge(y2_ps, b + 1)
                    dve.tensor_tensor(yn[:, :, G * D * g:G * D * (g + 1)].rearrange("p n (i d) -> p n i d", i=G),
                                      src[:, :, :, 0:D], rcp[:].unsqueeze(3).broadcast_to([P, TB, G, D]),
                                      ALU.mult).then_inc(y_norm, 1)
                if pos == PROJ_AT:
                    dve.wait_ge(proj_ps, ONE + b + 1)
                    dve.wait_ge(base_done, ONE + b + 1)
                    dve.wait_ge(out_stored[par], 16 * (half + 1))
                    dve.tensor_tensor(outb[:, par], ps[:, MISC, :].rearrange("p (n c) -> p n c", n=TB),
                                      base[:, par], ALU.add).then_inc(out_done, 1)

            timeline(dve, dve_at)

        @block.gpsimd
        def _(pool):
            pool.memset(probs[:], 0.0).then_inc(zero_made, 1)
            pool.iota(w8[:], pattern=[[-1, E]], base=E, channel_multiplier=0,
                      allow_small_or_imprecise_dtypes=True)
            pool.iota(jj[:], pattern=[[1, NST]], base=0, channel_multiplier=0,
                      allow_small_or_imprecise_dtypes=True).then_inc(iotas_made, 1)

            pool.wait_ge(proj_loaded, 16 * N_PROJ)
            pool.tensor_copy(wqk_dh[:].rearrange("p s (d h) -> p s d h", h=H),
                             wqkv[:, 0:2 * C].rearrange("p (s h d) -> p s d h", s=2, h=H)).then_inc(wqk_done, 1)

            def copy_x(b, par):
                pool.tensor_copy(xc[:, par, :], xnT[:, bass.ds(b * T, T)]).then_inc(xc_done, 1)

            for b in range(2):
                pool.wait_ge(xnT_done, b + 1)
                copy_x(b, b)

            pool.wait_ge(xn_done, NB)
            pool.wait_ge(slots_done, 1)
            pool.wait_ge(zero_stored, 16)
            for t in range(NT):
                pool.indirect_dma_start(xs_dram, bass.IndirectOffsetOnAxis(ap=slot[:, t:t + 1], axis=0),
                                        xn[:, t, :], None).then_inc(scattered, 16)

            def store_tile(q, r):
                pool.wait_ge(ye_done, FR * q + r + 1)
                pool.sem_inc(passed_pool, 1)
                pool.dma_start(ys_dram[bass.ds((FR * q + r) * P, P), :], yst[:, r, :]).then_inc(ys_stored[r], 16)

            sorted_tiles(pool, store_tile)
            for r in range(FR):
                pool.wait_ge(ys_stored[r], 16 * (NST // FR))
            pool.wait_ge(gate_done, 1)
            pool.wait_ge(small_loaded, 16 * N_SMALL)

            pool.sem_inc(base_done, ONE)

            def pool_at(b, half, par, pos):
                if pos == XC_AT and has(b + 2):
                    pool.wait_ge(v_ps, b + 1)
                    pool.sem_inc(passed_pool, 1)
                    copy_x(b + 2, par)
                for k in range(NG * TB):
                    if pos != ENDS[k] - 1:
                        continue
                    sb_ = k % TB
                    w = T - P * sb_
                    p = probs[:, P_AT[sb_]:P_AT[sb_] + G * w].rearrange("p (h w) -> p h w", h=G)[:, :, 0:P]
                    pool.wait_ge(exp_done, ST_RING + STEPS * b + ENDS[k])
                    pool.sem_inc(passed_pool, 1)
                    pool.affine_select(out=p, in_=p, compare_op=ALU.is_ge, fill=0.0, base=0,
                                       pattern=[[0, G], [1, P]], channel_multiplier=-1).then_inc(p_masked, 1)
                if pos == GATHER_AT:
                    pool.wait_ge(base_done, b + 1)
                    pool.sem_inc(passed_pool, 1)
                    pool.tensor_copy(slot_cur[:, par, :], slot[:, bass.ds(TB * b, TB)]).then_inc(idx_copied, 1)
                    pool.wait_ge(idx_copied, b + 1)
                    pool.sem_inc(passed_pool, 1)
                    for t in range(TB):
                        pool.indirect_dma_start(ysg[:, par, t, :], None, ys_dram,
                                                bass.IndirectOffsetOnAxis(ap=slot_cur[:, par, t:t + 1], axis=0)
                                                ).then_inc(gathered[par], 16)
                if pos == RESIDUAL_AT:
                    pool.wait_ge(gathered[par], 16 * TB * (half + 1))
                    pool.wait_ge(out_done, b + 1)
                    pool.tensor_tensor(ysg[:, par], ysg[:, par],
                                       gate[:, bass.ds(TB * b, TB)].unsqueeze(2).broadcast_to([P, TB, C]),
                                       ALU.mult).then_inc(gated, 1)
                    pool.tensor_tensor(base[:, par], xt[:, bass.ds(TB * b, TB), :],
                                       bpb[:].unsqueeze(1).broadcast_to([P, TB, C]), ALU.add).then_inc(biased, 1)
                    pool.wait_ge(gated, b + 1)
                    pool.wait_ge(biased, b + 1)
                    pool.tensor_tensor(base[:, par], base[:, par], ysg[:, par], ALU.add).then_inc(base_done, 1)

            timeline(pool, pool_at)

        @block.tensor
        def _(pe):
            pe.sem_inc(pv_done, P_RING)
            pe.sem_inc(yT_back, Y_RING)
            pe.sem_inc(y2_ps, ONE)
            pe.sem_inc(proj_ps, ONE)
            pe.wait_ge(const_loaded, 16 * N_CONST)

            def logits(b):
                pe.wait_ge(xnT_done, b + 1)
                for t in range(TB * b, TB * (b + 1)):
                    last = pe.matmul(ps[:, 2, t * E:(t + 1) * E], xnT[:, t * P:(t + 1) * P], wrt[:],
                                     start=True, stop=True)
                last.then_inc(logits_ps, 1)

            def project_qk(b, par, s, bank=MISC):
                pe.matmul(ps[:, bank, :], wqk_dh[:, s, :], xc[:, par, :], start=True, stop=True).then_inc(qk_ps, 1)

            def project_first(b):
                pe.wait_ge(wqk_done, 1)
                pe.wait_ge(xc_done, b + 1)
                if b:
                    pe.wait_ge(qk_copied, 2 * b)
                for s in range(2):
                    project_qk(b, b, s, QK_BANK[s])

            for b in range(NB):
                if b == 3:
                    project_first(0)
                if b == 5:
                    project_first(1)
                pe.wait_ge(xn_done, b + 1)
                if b >= 2:
                    pe.wait_ge(xnT_done, b - 1)
                for t in range(TB):
                    last = pe.transpose(ps[:, b % 2, t * P:(t + 1) * P], xn[:, TB * b + t, :], ident[:])
                last.then_inc(xnT_ps, 1)
                if b:
                    if b == 1:
                        pe.wait_ge(proj_loaded, 16 * N_PROJ)
                    logits(b - 1)
            logits(NB - 1)
            pe.wait_ge(small_loaded, 16 * N_SMALL)
            pe.transpose(ps[:, 3, 0:E * IC], b1r[:], ident[0:E * IC, 0:E * IC]).then_inc(b1_ps, 1)

            def project_v(b, par):
                for t in range(TB):
                    last = pe.matmul(ps[:, MISC, t * P:(t + 1) * P], xc[:, par, t * P:(t + 1) * P],
                                     wqkv[:, 2 * C:3 * C], start=True, stop=True)
                last.then_inc(v_ps, 1)

            def score_unit(b, half, par, g, u):
                tb, h0, nh = UNITS[u]
                w = P * (tb + 1)
                step = 2 * T // nh
                at = 64 * par
                if u == 0 and g == 0:
                    pe.wait_ge(stack_loaded[par], 16 * STACK_DMAS * (half + 1))
                pe.wait_ge(mx_done, NU * (NG * b + g) + u + 1)
                two = ps[:, S_BANK[u % 2]:S_BANK[u % 2] + 2, :].rearrange("p a t -> p (a t)")
                for n in range(nh):
                    h = G * g + h0 + n
                    pe.matmul(two[:, n * step:n * step + w],
                              stack[at:at + N_SCORE, 0, h, tb * P:(tb + 1) * P],
                              stack[at:at + N_SCORE, 1, h, 0:w], start=True, stop=False)
                    last = pe.matmul(two[:, n * step + w - P:n * step + w], ident_b, mask_b,
                                     start=False, stop=True)
                last.then_inc(s_ps, 1)

            def guard_back(b, pair):
                pe.wait_ge(mx_done, S_RING + NU * (NG * b + 2 * pair + 2))
                for tb in range(TB):
                    last = pe.transpose(ps[0:H // 2, MISC, tb * P:(tb + 1) * P],
                                        mx[:, tb, pair * H // 2:(pair + 1) * H // 2], ident[:])
                last.then_inc(guard_ps, 1)

            pe.wait_ge(onehot_done, 1)
            pe.wait_ge(b1_done, 1)
            oh2 = ohb[:].rearrange("p n e -> p (n e)")
            pe.matmul(ps[:, 3, 0:NT * E], tri_b, oh2, start=True, stop=True)
            pe.matmul(ps[:, 3, NT * E:2 * NT * E], ones_b, oh2, start=True, stop=True).then_inc(count_ps, 1)
            project_v(0, 0)
            pe.wait_ge(slots_done, 1)
            for g in range(LEAD):
                for u in range(NU):
                    score_unit(0, 0, 0, g, u)
                if g == 1:
                    pe.wait_ge(v_done, 1)
                    guard_back(0, 0)

            def tile_transpose(q, r):
                n = FR * q + r
                pe.wait_ge(xs_loaded[r], 16 * (q + 1))
                if not first(q):
                    pe.wait_ge(ye_done, n - FR + 1)
                pe.transpose(ps[:, r, 0:P], xst[:, r, :], ident[:]).then_inc(xsT_ps, 1)

            def tile_up(q, r):
                n = FR * q + r
                pe.wait_ge(xsT_done, n + 1)
                pe.wait_ge(wcur_done, n + 1)
                if not first(q):
                    pe.wait_ge(hid_done, IC * (n - FR + 1))
                for i in range(IC):
                    last = pe.matmul(ps[:, 3 + r, i * P:(i + 1) * P],
                                     wcur[:, r, W1_AT + i * P:W1_AT + (i + 1) * P], xsT[:, r, :],
                                     start=True, stop=True)
                last.then_inc(hid_ps, 1)

            def tile_down(q, r):
                for i in range(IC):
                    pe.wait_ge(hid_done, IC * (FR * q + r) + i + 1)
                    last = pe.matmul(ps[:, r, P:P + C], hid[:, r, i, :],
                                     wcur[:, r, W2_AT + i * C:W2_AT + (i + 1) * C],
                                     start=(i == 0), stop=(i == IC - 1))
                last.then_inc(ye_ps, 1)

            def tile_step(q, r):
                if not (final(q) and r == FR - 1):
                    tile_transpose(q + 1 if r == FR - 1 else q, (r + 1) % FR)
                tile_up(q, r)
                if not (first(q) and r == 0):
                    tile_down(q - 1 if r == 0 else q, (r - 1) % FR)

            pe.wait_ge(mx_done, S_RING + NU * LEAD)
            tile_transpose(0, 0)
            sorted_tiles(pe, tile_step)
            tile_down(NST // FR - 1, FR - 1)
            pe.wait_ge(ye_done, NST)
            pe.wait_ge(qk_copied, 4)
            pe.wait_ge(consts_made, 1)

            def pe_at(b, half, par, pos):
                at = 64 * par
                if pos < STEPS:
                    g, sb_, h0, nh = CHUNKS[pos]
                    w = T - P * sb_
                    if pos % (2 * GSTEPS) == 0:
                        pe.wait_ge(guard_loaded, 16 * (2 * b + 1 + pos // (2 * GSTEPS)))
                    pe.wait_ge(exp_done, STEPS * b + pos + 1)
                    for m in range(nh):
                        h = G * g + h0 + m
                        last = pe.matmul(ps[:, ST_BANK[pos % 2], m * w:(m + 1) * w],
                                         stack[at:at + N_STACK, 1, h, P * sb_:P * (sb_ + 1)],
                                         stack[at:at + N_STACK, 0, h, P * sb_:T], start=True, stop=True)
                    last.then_inc(st_ps, 1)
                unit = max_group(b, half, par, pos)
                if unit:
                    score_unit(*unit)
                for k in range(NG * TB):
                    if pos != weigh_at(k):
                        continue
                    g, sb_ = divmod(k, TB)
                    w = T - P * sb_
                    pe.wait_ge(p_masked, NG * TB * b + k + 1)
                    if sb_ == 0:
                        pe.wait_ge(yT_copied, NG * b + g + 1)
                        if g == 0:
                            pe.wait_ge(v_done, b + 1)
                    for m in range(G):
                        last = pe.matmul(ps[32 * m:32 * m + VW, PV_BANK, P * sb_:T],
                                         vt[:, par, sb_, G * g + m, :],
                                         probs[:, P_AT[sb_] + m * w:P_AT[sb_] + (m + 1) * w],
                                         start=(sb_ == 0), stop=(sb_ == TB - 1))
                    last.then_inc(pv_done, 1)

                pair = guard_pair(b, half, par, pos)
                if pair:
                    if pair[3] == 1:
                        pe.wait_ge(out_done, b + 1)
                    elif has(b + 2):
                        pe.wait_ge(qk_copied, 2 * (b + 2) + 2)
                    else:
                        pe.wait_ge(y_norm, NG * b + 2)
                    guard_back(pair[0], pair[3])
                if pos == V_AT and has(b + 1):
                    pe.wait_ge(y_norm, NG * b + 1)
                    project_v(b + 1, 1 - par)
                if pos == Q_AT and has(b + 2):
                    pe.wait_ge(v_done, b + 2)
                    pe.wait_ge(xc_done, b + 3)
                    project_qk(b + 2, par, 0)
                if pos == K_AT and has(b + 2):
                    pe.wait_ge(y_norm, NG * b + 2)
                    project_qk(b + 2, par, 1)
                for g in range(NG):
                    if pos != y_back_at(g):
                        continue
                    if g == 0:
                        pe.wait_ge(guard_left, 2 * b + 2)
                    elif g == 1 and has(b + 2):
                        pe.wait_ge(qk_copied, 2 * (b + 2) + 1)
                    elif g == 1 and has(b + 1):
                        pe.wait_ge(v_done, b + 2)
                    elif g == 2 and has(b + 1):
                        pe.wait_ge(guard_left, 2 * b + 3)
                    else:
                        pe.wait_ge(y_norm, NG * b + g)
                    pe.wait_ge(yT_copied, ONE + NG * b + g + 1)
                    for t in range(TB):
                        last = pe.transpose(ps[:, MISC, t * P:(t + 1) * P], yTs[:, g % 2, t * P:(t + 1) * P], ident[:])
                    last.then_inc(yT_back, 1)
                if pos == Y2_AT:
                    pe.wait_ge(y_norm, NG * b + NG)
                    for t in range(TB):
                        last = pe.transpose(ps[:, MISC, t * P:(t + 1) * P], yn[:, t, :], ident[:])
                    last.then_inc(y2_ps, 1)
                if pos == PROJ_AT:
                    pe.wait_ge(y2_copied, b + 1)
                    for t in range(TB):
                        last = pe.matmul(ps[:, MISC, t * C:(t + 1) * C], yn2[:, t * P:(t + 1) * P], wpj[:],
                                         start=True, stop=True)
                    last.then_inc(proj_ps, 1)

            timeline(pe, pe_at)


def top_bits(a):
    import numpy as np

    bits = np.ascontiguousarray(a, np.float32).view(np.uint32)
    kept = (bits & np.uint32(0xFFFF0000)).view(np.float32)
    return (bits >> np.uint32(16)).astype(np.uint16), (a - kept).astype(np.float32)


def shape_constants():
    import numpy as np

    pos = np.arange(T)
    slopes = (2.0 ** (-(8.0 / H) * np.arange(1, H + 1))).astype(np.float32)
    left = slopes[:, None] * pos[None, :].astype(np.float32)
    alibi = []
    for _ in range(N_ALIBI):
        part, left = top_bits(left)
        alibi.append(part)
    one = top_bits(np.ones((H, T), np.float32))[0]
    block = np.arange(CM)[:, None, None]
    before = top_bits(np.broadcast_to(np.where(pos[None, None] // 64 < block, -BIG, 0.0), (CM, H, T)).astype(np.float32))[0]
    inside = top_bits(np.broadcast_to(pos[None, None] // 64 == block, (CM, H, T)).astype(np.float32))[0]
    stack_q = np.concatenate([np.stack([one] * N_ALIBI), before])
    stack_k = np.concatenate([np.stack(alibi), inside, np.stack([one] * 3)])
    r = np.arange(P)
    bf = np.stack([np.eye(P), np.where(r[None] > r[:, None], -BIG, 0.0), r[:, None] < r[None], np.ones((P, P))], 1)
    return {"c_ident": np.eye(P, dtype=np.float32), "c_bf": top_bits(bf.astype(np.float32))[0],
            "c_stack_q": stack_q, "c_stack_k": stack_k}


_INS = ["L0_attn_x", "L0_attn_w_attn", "L0_attn_b_attn", "L0_attn_w_proj", "L0_attn_b_proj", "L0_ffn_w1",
        "L0_ffn_b1", "L0_ffn_w2", "L0_ffn_b2", "L0_ffn_wr", "L0_ffn_br"]


def kernel(**inputs):
    import numpy as np
    import concourse.bacc as bacc
    from concourse.bass_utils import run_bass_kernel_spmd

    nc = bacc.Bacc("TRN2", target_bir_lowering=False, num_devices=1)
    arrays = {name: np.ascontiguousarray(inputs[name]) for name in _INS}
    arrays.update(shape_constants())
    args = [nc.dram_tensor(name, a.shape, mybir.dt.from_np(a.dtype), kind="ExternalInput").ap()
            for name, a in arrays.items()]
    out = nc.dram_tensor("out", (NB, T, C), F32, kind="ExternalOutput").ap()
    block_kernel(nc, *args, out)
    return run_bass_kernel_spmd(nc, [arrays], core_ids=[0]).results[0]["out"]
```

```python
from contextlib import ExitStack

import concourse.bass as bass
from concourse import mybir

F32 = mybir.dt.float32
BF16 = mybir.dt.bfloat16
U16 = mybir.dt.uint16
U32 = mybir.dt.uint32
I32 = mybir.dt.int32
ALU = mybir.AluOpType
ACT = mybir.ActivationFunctionType
AX_X = mybir.AxisListType.X

P = 128
NB = 8
T = 512
C = 128
H = 16
D = C // H
TB = T // P
NT = NB * TB
E = 8
I = 512
IC = I // P
NST = NT + E - 1
EPS = 1e-5
BIG = 1e30
Q_SCALE = float(D) ** -0.5

W1_AT, B1_AT, W2_AT, B2_AT = 0, I, I + IC, I + IC + IC * C
WCOLS = B2_AT + C
FR = 3

PARTS_Q = (0, 0, 0, 1, 1, 2)
PARTS_K = (0, 1, 2, 0, 1, 0)
N_PROD = len(PARTS_Q) * D
N_ALIBI = 3
CM = T // 64
N_SCORE = N_PROD + N_ALIBI + CM
N_STACK = N_SCORE + 3

G = 4
NG = H // G
NY = NG // 2
VW = D + 1
V2 = 2 * VW


def score_chunks():
    out = []
    for g in range(NG):
        for sb in range(TB):
            nh = {0: 1, 1: 1, 2: 2, 3: 4}[sb]
            out += [(g, sb, h0, nh) for h0 in range(0, G, nh)]
    return out


def max_units():
    return [(3, 0, 2), (3, 2, 2), (2, 0, 2), (2, 2, 2), (1, 0, 4), (0, 0, 4)]


CHUNKS = score_chunks()
UNITS = max_units()
STEPS = len(CHUNKS)
GSTEPS = STEPS // NG
TAIL = 10
SPAN = STEPS + TAIL
NU = len(UNITS)
ENDS = {}
for _n, (_g, _sb, _h, _nh) in enumerate(CHUNKS):
    ENDS[TB * _g + _sb] = _n + 1

UNIT_AT = {0: 0, 2: 1, 4: 2, 5: 3, 7: 4, 9: 5}
LEAD = 3
GUARD_AT = {GSTEPS + 1: 1, 3 * GSTEPS: 2}
V_AT, Q_AT, K_AT = 16, 19, 29
LEFT_AT, MIDDLE_AT, LAST_AT = 2, 4, 6
XC_AT, PARTS_AT = 12, K_AT + LAST_AT + 1
SLOTS_AT, GATHER_AT = 13, (15, 16, 17, 19)
GATED_AT, BIASED_AT, BASE_AT = 26, 27, 28
Y2_AT, PROJ_AT = SPAN - 3, SPAN - 1


def weigh_at(k):
    return ENDS[k] + 2


def y_copy_at(y):
    return weigh_at(TB * (2 * y + 2) - 1) + 1


def y_back_at(y):
    return y_copy_at(y) + 2


P_AT = [G * sum(T - P * n for n in range(sb_)) for sb_ in range(TB)]
P_COLS = P_AT[-1] + G * P

STACK_DMAS = 7

ST_RING, P_RING, S_RING, Y_RING = 2, TB, 2, 2
ONE = 1


def block_kernel(nc, x, w_attn, b_attn, w_proj, b_proj, w1, b1, w2, b2, wr, br,
                 c_ident, c_bf, c_stack_q, c_stack_k, out):
    with ExitStack() as ctx:
        def sb(name, shape, dt=F32):
            return ctx.enter_context(nc.sbuf_tensor(name, shape, dt))

        def sem(name):
            return ctx.enter_context(nc.semaphore(name))

        xs_dram = nc.dram_tensor("xs_sorted", (NST * P, C), F32, kind="Internal").ap()
        ys_dram = nc.dram_tensor("ys_sorted", (NST * P, C), F32, kind="Internal").ap()
        parts_dram = nc.dram_tensor("qk_parts", (2, 2, 3, D, H, T), BF16, kind="Internal").ap()
        guard_dram = nc.dram_tensor("guard_parts", (2, 3, H // 2, T), BF16, kind="Internal").ap()

        xt = sb("xt", [P, NT, C])
        xn = sb("xn", [P, NT, C])
        xnT = sb("xnT", [P, NT * P])
        wall = sb("wall", [P, E, WCOLS])
        wcur = sb("wcur", [P, FR, WCOLS])
        stack = sb("stack", [P, 2, H, T], BF16)
        probs = sb("probs", [P, P_COLS])
        vt = sb("vt", [P, 2, TB, H, V2])
        xc = sb("xc", [P, 2, T])
        qkr = sb("qkr", [P, 2, T])
        qkp = sb("qkp", [P, 2, 3, T], BF16)
        yn = sb("yn", [P, TB, C])
        yn2 = sb("yn2", [P, T])
        rcp = sb("rcp", [P, TB, G, 2])
        mx = sb("mx", [P, TB, H])
        guard_r = sb("guard_r", [P, P])
        guard_p = sb("guard_p", [P, 3, P], BF16)
        reuse = xn[:].rearrange("p (b q n) c -> p b q n c", b=4, q=2)
        ysg, base, outb, yTq = (reuse[:, n] for n in range(4))
        yTs = yTq.rearrange("p q n c -> p q (n c)")
        slot_cur = sb("slot_cur", [P, 2, TB], U32)
        xst = sb("xst", [P, FR, C])
        xsT = sb("xsT", [P, FR, P])
        hid = sb("hid", [P, FR, IC, P])
        yst = sb("yst", [P, FR, C])
        wqkv = sb("wqkv", [P, 3 * C])
        wqk_dh = sb("wqk_dh", [P, 2, C])
        wpj = sb("wpj", [P, C])
        wrt = sb("wrt", [P, E])
        bqk = sb("bqk", [P, 2])
        bqk_s = sb("bqk_s", [P, 2])
        bvb = sb("bvb", [P, C])
        bpb = sb("bpb", [P, C])
        brb = sb("brb", [P, E])
        b1r = sb("b1r", [E * IC, P])
        ident = sb("ident", [P, P])
        cbf = sb("cbf", [P, 4, P], BF16)
        ident_b, mask_b, tri_b, ones_b = (cbf[:, n, :] for n in range(4))
        bst = sb("bst", [P, NT, 6])
        mv = sb("mv", [P, NT, 2])
        std = sb("std", [P, NT])
        rstd = sb("rstd", [P, NT])
        eps = sb("eps", [P, 1])
        tmp = wcur[:].rearrange("p r w -> p (r w)")
        lg, lg2, eqw, oh = (tmp[:, n * NT * E:(n + 1) * NT * E].rearrange("p (n e) -> p n e", e=E) for n in range(4))
        cnt, csum, rank_f = (tmp[:, n * NT * E:(n + 1) * NT * E] for n in range(4, 7))
        rank = rank_f.rearrange("p (e n) -> p e n", e=E)
        cmp = tmp[:, 7 * NT * E:7 * NT * E + NST * E].rearrange("p (j e) -> p j e", e=E)
        ohb = sb("ohb", [P, NT, E], BF16)
        w8 = sb("w8", [P, E])
        mx1 = sb("mx1", [P, NT])
        mxw = sb("mxw", [P, NT])
        mx2 = sb("mx2", [P, NT])
        dgap = sb("dgap", [P, NT])
        gexp = sb("gexp", [P, NT])
        gate = sb("gate", [P, NT])
        ones_f = sb("ones_f", [P, E * NT])
        bef = sb("bef", [P, E + 1])
        npe = sb("npe", [P, E])
        npi = sb("npi", [P, E], I32)
        nti = sb("nti", [P, E], I32)
        ntl = sb("ntl", [P, E])
        tinc = sb("tinc", [P, E])
        tex = sb("tex", [P, E])
        dlt = sb("dlt", [P, E])
        slotf = sb("slotf", [P, NT])
        slot = sb("slot", [P, NT], U32)
        jj = sb("jj", [P, NST])
        ef = sb("ef", [P, NST])
        eidx = sb("eidx", [P, NST], I32)

        ps = ctx.enter_context(nc.psum_tensor("ps", [P, 8, T], F32))
        S_BANK = (0, 2)
        ST_BANK = (4, 5)
        PV_BANK, MISC = 6, 7
        QK_BANK = (4, 5)

        x_loaded = [sem(f"x_loaded{b}") for b in range(NB)]
        small_loaded = sem("small_loaded")
        const_loaded = sem("const_loaded")
        proj_loaded = sem("proj_loaded")
        rows_loaded = sem("rows_loaded")
        w1_loaded = sem("w1_loaded")
        zero_made = sem("zero_made")
        zero_stored = sem("zero_stored")
        consts_made = sem("consts_made")
        vt_made = sem("vt_made")
        iotas_made = sem("iotas_made")
        dve_chain = sem("dve_chain")
        stats_done = sem("stats_done")
        std_done = sem("std_done")
        rstd_done = sem("rstd_done")
        xn_done = sem("xn_done")
        xn_last_done = sem("xn_last_done")
        xnT_ps = sem("xnT_ps")
        xnT_done = sem("xnT_done")
        b1_ps = sem("b1_ps")
        b1_done = sem("b1_done")
        logits_ps = sem("logits_ps")
        onehot_done = sem("onehot_done")
        count_ps = sem("count_ps")
        gap_done = sem("gap_done")
        gexp_done = sem("gexp_done")
        gate_done = sem("gate_done")
        slots_done = sem("slots_done")
        experts_known = sem("experts_known")
        scattered = sem("scattered")
        bias_scaled = sem("bias_scaled")
        xs_loaded = [sem(f"xs_loaded{r}") for r in range(FR)]
        wcur_done = sem("wcur_done")
        xsT_ps = sem("xsT_ps")
        xsT_done = sem("xsT_done")
        hid_ps = sem("hid_ps")
        hid_done = sem("hid_done")
        ye_ps = sem("ye_ps")
        ye_done = sem("ye_done")
        ys_stored = [sem(f"ys_stored{r}") for r in range(FR)]
        wqk_done = sem("wqk_done")
        xc_done = sem("xc_done")
        qk_ps = sem("qk_ps")
        qk_copied = sem("qk_copied")
        qk_left = sem("qk_left")
        qk_middle = sem("qk_middle")
        qk_split = sem("qk_split")
        parts_stored = sem("parts_stored")
        stack_loaded = [sem(f"stack_loaded{p}") for p in range(2)]
        v_ps = sem("v_ps")
        v_done = sem("v_done")
        s_ps = sem("s_ps")
        mx_done = sem("mx_done")
        guard_ps = sem("guard_ps")
        guard_first = sem("guard_first")
        guard_left = sem("guard_left")
        guard_middle = sem("guard_middle")
        guard_split = sem("guard_split")
        dve_passed, pool_passed = sem("dve_passed"), sem("pool_passed")
        guard_stored = sem("guard_stored")
        guard_loaded = sem("guard_loaded")
        st_ps = sem("st_ps")
        exp_done = sem("exp_done")
        p_masked = sem("p_masked")
        pv_done = sem("pv_done")
        yT_copied = sem("yT_copied")
        yT_back = sem("yT_back")
        rcp_done = sem("rcp_done")
        y_norm = sem("y_norm")
        y2_ps = sem("y2_ps")
        y2_copied = sem("y2_copied")
        proj_ps = sem("proj_ps")
        idx_copied = sem("idx_copied")
        gathered = [sem(f"gathered{p}") for p in range(2)]
        gated = sem("gated")
        biased = sem("biased")
        base_done = sem("base_done")
        out_done = sem("out_done")
        out_stored = [sem(f"out_stored{p}") for p in range(2)]

        N_SMALL, N_CONST, N_PROJ, N_ROWS = 7, 2, 2, 4

        def timeline(eng, at):
            def window(b, half, par, following):
                for pos in range(TAIL, SPAN):
                    at(b, half, par, pos)
                    if pos >= STEPS and following:
                        at(b + 1, half + par, 1 - par, pos - STEPS)

            for pos in range(TAIL):
                at(0, 0, 0, pos)
            with eng.Fori(0, (NB - 2) // 2) as i:
                for par in range(2):
                    window(2 * i + par, i, par, True)
            for b in (NB - 2, NB - 1):
                window(b, b // 2, b % 2, b + 1 < NB)

        def has(b):
            return not isinstance(b, int) or b < NB

        def max_group(b, half, par, pos):
            if pos >= STEPS or pos % GSTEPS not in UNIT_AT:
                return None
            g = pos // GSTEPS + LEAD
            if g >= NG:
                b, half, par, g = b + 1, half + par, 1 - par, g - NG
            return (b, half, par, g, UNIT_AT[pos % GSTEPS]) if has(b) else None

        def guard_pair(b, half, par, pos):
            if pos not in GUARD_AT:
                return None
            if GUARD_AT[pos] == 1:
                return b, half, par, 1
            return (b + 1, half + par, 1 - par, 0) if has(b + 1) else None

        def sorted_tiles(eng, body):
            for r in range(FR):
                body(0, r)
            with eng.Fori(1, NST // FR - 1) as q:
                for r in range(FR):
                    body(q, r)
            for r in range(FR):
                body(NST // FR - 1, r)

        def first(q):
            return isinstance(q, int) and q == 0

        def final(q):
            return isinstance(q, int) and q == NST // FR - 1

        block = ctx.enter_context(nc.Block())

        @block.sync
        def _(sp):
            for par in range(2):
                sp.sem_inc(out_stored[par], 16 * ONE)
            for b in range(NB):
                sp.dma_start(xt[:, TB * b:TB * (b + 1), :],
                             x[b].rearrange("(n p) c -> p n c", p=P)).then_inc(x_loaded[b], 16)
            sp.dma_start(bvb[:], b_attn[2 * C:3 * C].partition_broadcast(P)).then_inc(small_loaded, 16)
            sp.dma_start(bpb[:], b_proj.partition_broadcast(P)).then_inc(small_loaded, 16)
            sp.dma_start(brb[:], br.partition_broadcast(P)).then_inc(small_loaded, 16)
            sp.dma_start(b1r[:], b1.rearrange("e (i p) -> (e i) p", p=P)).then_inc(small_loaded, 16)
            sp.dma_start(wpj[:], w_proj).then_inc(small_loaded, 16)
            for par in range(2):
                at = 64 * par
                sp.dma_start(stack[at + N_PROD:at + N_SCORE, 0].bitcast(U16), c_stack_q).then_inc(rows_loaded, 16)
                sp.dma_start(stack[at + N_PROD:at + N_STACK, 1].bitcast(U16), c_stack_k).then_inc(rows_loaded, 16)
            sp.wait_ge(zero_made, 1)
            zeros = probs[:, 0:NST * C]
            sp.dma_start(xs_dram.rearrange("(p n) c -> p (n c)", p=P), zeros).then_inc(zero_stored, 16)

            for e in range(E):
                sp.dma_start(wall[:, e, W1_AT:W1_AT + I], w1[e]).then_inc(w1_loaded, 16)
                sp.dma_start(wall[:, e, W2_AT:W2_AT + IC * C].rearrange("p (i c) -> p i c", i=IC),
                             w2[e].rearrange("(i p) c -> p i c", p=P)).then_inc(w1_loaded, 16)
                sp.dma_start(wall[:, e, B2_AT:B2_AT + C], b2[e].partition_broadcast(P)).then_inc(w1_loaded, 16)

            def store_parts(b, par):
                for s in range(2):
                    sp.wait_ge(qk_split, 2 * b + s + 1)
                    sp.dma_start(parts_dram[par, s].rearrange("j d h t -> (d h) j t"),
                                 qkp[:, s]).then_inc(parts_stored, 16)
                sp.wait_ge(parts_stored, 32 * b + 32)

            def load_stack(par):
                at = 64 * par

                def one(s, row, first_part, n_parts):
                    dst = stack[at + D * row:at + D * (row + n_parts), s]
                    src = parts_dram[par, s, first_part:first_part + n_parts]
                    sp.dma_start(dst, src.rearrange("j d h t -> (j d) h t")).then_inc(stack_loaded[par], 16)

                for s, parts in ((0, PARTS_Q), (1, PARTS_K)):
                    row = 0
                    while row < len(parts):
                        n = 1
                        while row + n < len(parts) and parts[row + n] == parts[row] + n:
                            n += 1
                        one(s, row, parts[row], n)
                        row += n

            def load_guard(b, par, pair):
                n = 2 * b + pair + 1
                sp.wait_ge(guard_split, n)
                for tb in range(TB):
                    sp.dma_start(guard_dram[pair, :, :, tb * P:(tb + 1) * P].rearrange("j h t -> h j t"),
                                 guard_p[32 * tb:32 * tb + H // 2]).then_inc(guard_stored, 16)
                sp.wait_ge(guard_stored, 16 * TB * n)
                row = 64 * par + N_SCORE
                sp.dma_start(stack[row:row + 3, 0, pair * H // 2:(pair + 1) * H // 2, :], guard_dram[pair]
                             ).then_inc(guard_loaded, 16)

            for b in range(2):
                store_parts(b, b)
                if b == 0:
                    sp.wait_ge(rows_loaded, 16 * N_ROWS)
                load_stack(b)
            load_guard(0, 0, 0)
            sp.wait_ge(scattered, 16 * NT)

            def load_tile(q, r):
                if not first(q):
                    sp.wait_ge(xsT_ps, FR * (q - 1) + r + 1)
                sp.dma_start(xst[:, r, :], xs_dram[bass.ds((FR * q + r) * P, P), :]).then_inc(xs_loaded[r], 16)

            sorted_tiles(sp, load_tile)

            def io_at(b, half, par, pos):
                pair = guard_pair(b, half, par, pos)
                if pair:
                    load_guard(pair[0], pair[2], pair[3])
                if pos == PARTS_AT and has(b + 2):
                    store_parts(b + 2, par)
                if pos == STEPS and has(b + 2):
                    sp.wait_ge(st_ps, STEPS * b + STEPS)
                    load_stack(par)
                if pos == PROJ_AT:
                    sp.wait_ge(out_done, ONE + b + 1)
                    dst = out[bass.ds(b, 1), :, :].rearrange("o (n p) c -> p (o n) c", p=P)
                    sp.dma_start(dst, outb[:, par]).then_inc(out_stored[par], 16)

            timeline(sp, io_at)
            for par in range(2):
                sp.wait_ge(out_stored[par], 16 * (ONE + NB // 2))

        @block.scalar
        def _(act):
            act.dma_start(ident[:], c_ident).then_inc(const_loaded, 16)
            act.dma_start(cbf[:].bitcast(U16), c_bf).then_inc(const_loaded, 16)
            act.dma_start(wqkv[:], w_attn).then_inc(proj_loaded, 16)
            act.dma_start(wrt[:], wr).then_inc(proj_loaded, 16)
            for s in range(2):
                act.dma_start(bqk[:, s:s + 1], b_attn[s * C:(s + 1) * C].rearrange("(h d o) -> d h o", d=D, o=1),
                              allow_slow_non_contiguous=True).then_inc(small_loaded, 16)
            act.sem_inc(exp_done, ST_RING)
            act.sem_inc(yT_copied, ONE)

            def copy_qk(b, s, bank=MISC):
                if s == 0 and not (isinstance(b, int) and b == 0):
                    act.wait_ge(qk_split, 2 * b)
                    act.wait_ge(parts_stored, 32 * b)
                act.wait_ge(qk_ps, 2 * b + s + 1)
                act.activation(qkp[:, s, 0, :], ps[:, bank, :], ACT.Identity, bias=bqk_s[:, s:s + 1]
                               ).then_inc(qk_copied, 1)

            def middle_qk(b, s):
                act.wait_ge(qk_left, 2 * b + s + 1)
                act.copy(qkp[:, s, 1, :], qkr[:, s, :]).then_inc(qk_middle, 1)

            def guard_high(n):
                act.wait_ge(guard_ps, n + 1)
                if not (isinstance(n, int) and n == 0):
                    act.wait_ge(guard_loaded, 16 * n)
                act.mul(guard_p[:, 0, :], ps[:, MISC, 0:P], -1.0).then_inc(guard_first, 1)

            def guard_mid(n):
                act.wait_ge(guard_left, n + 1)
                act.copy(guard_p[:, 1, :], guard_r[:]).then_inc(guard_middle, 1)

            for b in range(NB + 2):
                if b < NB:
                    act.wait_ge(stats_done, b + 1)
                    act.activation(std[:, TB * b:TB * (b + 1)], mv[:, TB * b:TB * (b + 1), 1], ACT.Sqrt,
                                   bias=eps[:]).then_inc(std_done, 1)
                b -= 2
                if b < 0:
                    continue
                act.wait_ge(xnT_ps, b + 1)
                if b < 2:
                    act.copy(xc[:, b, :], ps[:, b % 2, :]).then_inc(xc_done, 1)
                act.copy(xnT[:, b * T:(b + 1) * T], ps[:, b % 2, :]).then_inc(xnT_done, 1)
            act.wait_ge(small_loaded, 16 * N_SMALL)
            act.mul(bqk_s[:, 0:1], bqk[:, 0:1], Q_SCALE).then_inc(bias_scaled, 1)
            act.copy(bqk_s[:, 1:2], bqk[:, 1:2]).then_inc(bias_scaled, 1)
            act.wait_ge(bias_scaled, 2)
            for s in range(2):
                copy_qk(0, s, QK_BANK[s])
            act.wait_ge(b1_ps, 1)
            act.copy(wall[:, :, B1_AT:B1_AT + IC], ps[:, 3, 0:E * IC].rearrange("p (e i) -> p e i", e=E)
                     ).then_inc(b1_done, 1)
            for s in range(2):
                middle_qk(0, s)
            act.wait_ge(gap_done, 1)
            act.activation(gexp[:], dgap[:], ACT.Exp).then_inc(gexp_done, 1)
            for s in range(2):
                copy_qk(1, s, QK_BANK[s])
            for s in range(2):
                middle_qk(1, s)
            guard_high(0)
            guard_mid(0)

            def tile_act(q, r):
                n = FR * q + r
                act.wait_ge(xsT_ps, n + 1)
                if not first(q):
                    act.wait_ge(hid_ps, n - FR + 1)
                act.copy(xsT[:, r, :], ps[:, r, 0:P]).then_inc(xsT_done, 1)

            def tile_gelu(q, r):
                n = FR * q + r
                act.wait_ge(hid_ps, n + 1)
                if not first(q):
                    act.wait_ge(ye_ps, n - FR + 1)
                for i in range(IC):
                    act.activation(hid[:, r, i, :], ps[:, 3 + r, i * P:(i + 1) * P], ACT.Gelu,
                                   bias=wcur[:, r, B1_AT + i:B1_AT + i + 1]).then_inc(hid_done, 1)

            def tile_pair(q, r):
                if not (final(q) and r == FR - 1):
                    tile_act(q + 1 if r == FR - 1 else q, (r + 1) % FR)
                tile_gelu(q, r)

            tile_act(0, 0)
            sorted_tiles(act, tile_pair)

            act.wait_ge(zero_stored, 16)

            def act_at(b, half, par, pos):
                if pos < STEPS:
                    g, sb_, h0, nh = CHUNKS[pos]
                    w = T - P * sb_
                    if h0 == 0:
                        act.wait_ge(pv_done, NG * TB * b + TB * g + sb_ + 1)
                    act.wait_ge(st_ps, STEPS * b + pos + 1)
                    at = P_AT[sb_] + h0 * w
                    act.activation(probs[:, at:at + nh * w].rearrange("p (h w) -> p h w", h=nh),
                                   ps[:, ST_BANK[pos % 2], 0:nh * w].rearrange("p (h w) -> p h w", h=nh),
                                   ACT.Exp).then_inc(exp_done, 1)
                for y in range(NY):
                    if pos == y_copy_at(y):
                        act.wait_ge(pv_done, P_RING + TB * (NG * b + 2 * y + 2))
                        act.wait_ge(yT_back, NY * b + y + 1)
                        act.copy(yTs[:, y, :], ps[:, PV_BANK, :]).then_inc(yT_copied, 1)
                for s, at in enumerate((Q_AT, K_AT)):
                    if pos == at + 1 and has(b + 2):
                        copy_qk(b + 2, s)
                    if pos == at + MIDDLE_AT and has(b + 2):
                        middle_qk(b + 2, s)
                pair = guard_pair(b, half, par, pos)
                if pair:
                    guard_high(2 * pair[0] + pair[3])
                pair = guard_pair(b, half, par, pos - 1)
                if pair:
                    guard_mid(2 * pair[0] + pair[3])
                if pos == Y2_AT:
                    act.wait_ge(proj_ps, b + 1)
                    act.wait_ge(y2_ps, ONE + b + 1)
                    act.copy(yn2[:], ps[:, MISC, :]).then_inc(y2_copied, 1)

            timeline(act, act_at)

        @block.vector
        def _(dve):
            chain = [0]

            def then(ins):
                chain[0] += 1
                ins.then_inc(dve_chain, 1)
                dve.wait_ge(dve_chain, chain[0])

            dve.memset(ones_f[:], 1.0)
            dve.memset(bef[:, 0:1], 0.0)
            dve.memset(eps[:], EPS)
            dve.memset(ps[:, PV_BANK, :], 0.0).then_inc(consts_made, 1)
            dve.sem_inc(mx_done, S_RING)
            dve.sem_inc(out_done, ONE)

            def normalise(b):
                dve.wait_ge(std_done, b + 1)
                dve.reciprocal(rstd[:, TB * b:TB * (b + 1)], std[:, TB * b:TB * (b + 1)]).then_inc(rstd_done, 1)
                dve.wait_ge(rstd_done, b + 1)
                for t in range(TB * b, TB * (b + 1) - 1):
                    last = dve.tensor_scalar(xn[:, t, :], xt[:, t, :], mv[:, t, 0:1], rstd[:, t:t + 1],
                                             ALU.subtract, ALU.mult)
                last.then_inc(xn_done, 1)

            for b in range(NB):
                dve.wait_ge(x_loaded[b], 16)
                for t in range(TB * b, TB * (b + 1)):
                    last = dve.bn_stats(bst[:, t, :], xt[:, t, :])
                then(last)
                for t in range(TB * b, TB * (b + 1)):
                    last = dve.bn_aggr(mv[:, t, :], bst[:, t, :])
                last.then_inc(stats_done, 1)
                if b:
                    normalise(b - 1)
            normalise(NB - 1)

            def split_qk(b, s, bank=MISC):
                dve.wait_ge(qk_copied, 2 * b + s + 1)
                dve.scalar_tensor_tensor(qkr[:, s, :], ps[:, bank, :], bqk_s[:, s:s + 1], qkp[:, s, 0, :],
                                         ALU.add, ALU.subtract).then_inc(qk_left, 1)

            def last_qk(b, s):
                dve.wait_ge(qk_middle, 2 * b + s + 1)
                dve.tensor_tensor(qkp[:, s, 2, :], qkr[:, s, :], qkp[:, s, 1, :], ALU.subtract).then_inc(qk_split, 1)

            def over_e(ap):
                return ap.unsqueeze(2).broadcast_to([P, NT, E])

            dve.wait_ge(logits_ps, NB)
            dve.wait_ge(small_loaded, 16 * N_SMALL)
            dve.wait_ge(iotas_made, 1)
            then(dve.tensor_tensor(lg, ps[:, 2, 0:NT * E].rearrange("p (n e) -> p n e", e=E),
                                   brb[:].unsqueeze(1).broadcast_to([P, NT, E]), ALU.add))
            then(dve.tensor_reduce(mx1[:], lg, AX_X, ALU.max))
            then(dve.tensor_tensor(eqw, lg, over_e(mx1[:]), ALU.is_equal))
            then(dve.tensor_tensor(eqw, eqw, w8[:].unsqueeze(1).broadcast_to([P, NT, E]), ALU.mult))
            then(dve.tensor_reduce(mxw[:], eqw, AX_X, ALU.max))
            then(dve.tensor_tensor(oh, eqw, over_e(mxw[:]), ALU.is_equal))
            dve.tensor_copy(ohb[:], oh).then_inc(onehot_done, 1)
            then(dve.scalar_tensor_tensor(lg2, oh, -BIG, lg, ALU.mult, ALU.add))
            then(dve.tensor_reduce(mx2[:], lg2, AX_X, ALU.max))
            dve.tensor_tensor(dgap[:], mx2[:], mx1[:], ALU.subtract).then_inc(gap_done, 1)

            for s in range(2):
                split_qk(0, s, QK_BANK[s])

            dve.wait_ge(count_ps, 1)
            pre = ps[:, 3, 0:NT * E].rearrange("p (n e) -> p e n", e=E)
            tot = ps[:, 3, NT * E:2 * NT * E].rearrange("p (n e) -> p e n", e=E)
            then(dve.tensor_copy(cnt.rearrange("p (e n) -> p e n", e=E), tot))
            then(dve.tensor_tensor_scan(csum, ones_f[:], cnt, 0.0, ALU.mult, ALU.add))
            then(dve.tensor_copy(bef[:, 1:E + 1], csum.rearrange("p (e n) -> p e n", e=E)[:, :, NT - 1]))
            then(dve.tensor_tensor(npe[:], bef[:, 1:E + 1], bef[:, 0:E], ALU.subtract))
            then(dve.tensor_scalar(npi[:], npe[:], float(P - 1), None, ALU.add))
            then(dve.tensor_single_scalar(nti[:], npi[:], P.bit_length() - 1, ALU.arith_shift_right))
            then(dve.tensor_copy(ntl[:], nti[:]))
            then(dve.tensor_tensor_scan(tinc[:], ones_f[:, 0:E], ntl[:], 0.0, ALU.mult, ALU.add))
            then(dve.tensor_tensor(tex[:], tinc[:], ntl[:], ALU.subtract))
            then(dve.scalar_tensor_tensor(dlt[:], tex[:], float(P), bef[:, 0:E], ALU.mult, ALU.subtract))
            then(dve.tensor_tensor(csum, csum, cnt, ALU.subtract))
            then(dve.tensor_tensor(rank, csum.rearrange("p (e n) -> p e n", e=E), pre, ALU.add))
            then(dve.tensor_tensor(rank, rank, dlt[:].unsqueeze(2).broadcast_to([P, E, NT]), ALU.add))
            then(dve.tensor_tensor(rank, rank, oh.rearrange("p n e -> p e n"), ALU.mult))
            then(dve.tensor_reduce(slotf[:], rank.rearrange("p e n -> p n e"), AX_X, ALU.add))
            dve.tensor_copy(slot[:], slotf[:]).then_inc(slots_done, 1)
            for s in range(2):
                last_qk(0, s)
            then(dve.tensor_tensor(cmp, jj[:].unsqueeze(2).broadcast_to([P, NST, E]),
                                   tex[:].unsqueeze(1).broadcast_to([P, NST, E]), ALU.is_ge))
            then(dve.tensor_reduce(ef[:], cmp, AX_X, ALU.add))
            then(dve.tensor_scalar(ef[:], ef[:], -1.0, None, ALU.add))
            dve.tensor_copy(eidx[:], ef[:]).then_inc(experts_known, 1)
            dve.wait_ge(gexp_done, 1)
            then(dve.tensor_scalar(gexp[:], gexp[:], 1.0, None, ALU.add))
            dve.reciprocal(gate[:], gexp[:]).then_inc(gate_done, 1)
            for s in range(2):
                split_qk(1, s, QK_BANK[s])
            for s in range(2):
                last_qk(1, s)

            def copy_v(b, par):
                dve.wait_ge(v_ps, b + 1)
                for g in range(NG):
                    at = (g % 2) * VW
                    last = dve.tensor_tensor(vt[:, par, :, G * g:G * (g + 1), at:at + D],
                                             ps[:, MISC, :].rearrange("p (n h d) -> p n h d", n=TB, h=H)
                                             [:, :, G * g:G * (g + 1), :],
                                             bvb[:].rearrange("p (h d) -> p h d", h=H)[:, G * g:G * (g + 1), :]
                                             .unsqueeze(1).broadcast_to([P, TB, G, D]), ALU.add)
                last.then_inc(v_done, 1)

            def row_max(b, g, u):
                tb, h0, nh = UNITS[u]
                w = P * (tb + 1)
                two = ps[:, S_BANK[u % 2]:S_BANK[u % 2] + 2, :].rearrange("p a t -> p (a t)")
                src = two.rearrange("p (h w) -> p h w", h=nh)[:, :, 0:w]
                dve.wait_ge(s_ps, NU * (NG * b + g) + u + 1)
                if u == 0 and g % 2 == 0 and not (isinstance(b, int) and b == 0):
                    dve.wait_ge(guard_ps, 2 * b - 1 + g // 2)
                dve.tensor_reduce(mx[:, tb, G * g + h0:G * g + h0 + nh], src, AX_X, ALU.max).then_inc(mx_done, 1)

            def guard_rest(n):
                dve.wait_ge(guard_first, n + 1)
                dve.scalar_tensor_tensor(guard_r[:], ps[:, MISC, 0:P], -1.0, guard_p[:, 0, :],
                                         ALU.mult, ALU.subtract).then_inc(guard_left, 1)

            def guard_last(n):
                dve.wait_ge(guard_middle, n + 1)
                dve.tensor_tensor(guard_p[:, 2, :], guard_r[:], guard_p[:, 1, :], ALU.subtract
                                  ).then_inc(guard_split, 1)

            dve.wait_ge(vt_made, 3)
            copy_v(0, 0)
            for g in range(LEAD):
                for u in range(NU):
                    row_max(0, g, u)
                if g == 1:
                    guard_rest(0)
                    guard_last(0)

            def expert_of(q, r):
                return dve.value_load(eidx[0:1, bass.ds(FR * q + r, 1)], min_val=0, max_val=E - 1)

            def expert_weights(e, r):
                dve.tensor_copy(wcur[:, r, :], wall[:, bass.ds(e, 1), :].rearrange("p o w -> p (o w)")
                                ).then_inc(wcur_done, 1)

            dve.wait_ge(w1_loaded, 16 * 3 * E)
            dve.wait_ge(b1_done, 1)
            dve.wait_ge(experts_known, 1)
            for r in range(FR):
                expert_weights(expert_of(0, r), r)

            def tile_y(q, r):
                if not final(q):
                    e = expert_of(q + 1, r)
                dve.wait_ge(ye_ps, FR * q + r + 1)
                if not first(q):
                    dve.wait_ge(ys_stored[r], 16 * q)
                dve.tensor_tensor(yst[:, r, :], ps[:, r, P:P + C], wcur[:, r, B2_AT:B2_AT + C],
                                  ALU.add).then_inc(ye_done, 1)
                if not final(q):
                    dve.wait_ge(ye_done, FR * q + r + 1)
                    dve.sem_inc(dve_passed, 1)
                    expert_weights(e, r)

            sorted_tiles(dve, tile_y)

            def dve_at(b, half, par, pos):
                unit = max_group(b, half, par, pos)
                if unit:
                    row_max(unit[0], unit[3], unit[4])
                pair = guard_pair(b, half, par, pos)
                if pair:
                    guard_rest(2 * pair[0] + pair[3])
                pair = guard_pair(b, half, par, pos - 1)
                if pair:
                    guard_last(2 * pair[0] + pair[3])
                for s, at in enumerate((Q_AT, K_AT)):
                    if pos == at + LEFT_AT and has(b + 2):
                        split_qk(b + 2, s)
                    if pos == at + LAST_AT and has(b + 2):
                        last_qk(b + 2, s)
                if pos == V_AT and has(b + 1):
                    copy_v(b + 1, 1 - par)
                for y in range(NY):
                    if pos != y_back_at(y):
                        continue
                    src = ps[:, MISC, 0:TB * G * V2].rearrange("p (n i q j) -> p n i q j", n=TB, i=G, q=2)
                    dve.wait_ge(yT_back, NY * b + y + 1 + Y_RING)
                    dve.reciprocal(rcp[:], src[:, :, :, :, D]).then_inc(rcp_done, 1)
                    dve.wait_ge(rcp_done, NY * b + y + 1)
                    if y == 0:
                        dve.wait_ge(y2_ps, b + 1)
                    for q in range(2):
                        g = 2 * y + q
                        last = dve.tensor_tensor(yn[:, :, G * D * g:G * D * (g + 1)]
                                                 .rearrange("p n (i d) -> p n i d", i=G),
                                                 src[:, :, :, q, 0:D],
                                                 rcp[:, :, :, q].unsqueeze(3).broadcast_to([P, TB, G, D]), ALU.mult)
                    last.then_inc(y_norm, 1)
                if pos == PROJ_AT:
                    dve.wait_ge(proj_ps, ONE + b + 1)
                    dve.wait_ge(base_done, ONE + b + 1)
                    dve.wait_ge(out_stored[par], 16 * (half + 1))
                    dve.tensor_tensor(outb[:, par], ps[:, MISC, :].rearrange("p (n c) -> p n c", n=TB),
                                      base[:, par], ALU.add).then_inc(out_done, 1)

            timeline(dve, dve_at)

        @block.gpsimd
        def _(pool):
            pool.memset(probs[:], 0.0).then_inc(zero_made, 1)
            pool.iota(w8[:], pattern=[[-1, E]], base=E, channel_multiplier=0,
                      allow_small_or_imprecise_dtypes=True)
            pool.iota(jj[:], pattern=[[1, NST]], base=0, channel_multiplier=0,
                      allow_small_or_imprecise_dtypes=True).then_inc(iotas_made, 1)

            pool.memset(vt[:], 0.0).then_inc(vt_made, 1)
            pool.wait_ge(vt_made, 1)
            v_of = vt[:].rearrange("p a n (y q m) w -> p (a n y) q m w", y=NY, q=2)
            for q in range(2):
                pool.memset(v_of[:, :, q, :, q * VW + D], 1.0).then_inc(vt_made, 1)

            pool.wait_ge(proj_loaded, 16 * N_PROJ)
            pool.tensor_scalar(wqk_dh[:, 0].rearrange("p (d h) -> p d h", h=H),
                               wqkv[:, 0:C].rearrange("p (h d) -> p d h", h=H), Q_SCALE, None, ALU.mult
                               ).then_inc(wqk_done, 1)
            pool.tensor_copy(wqk_dh[:, 1].rearrange("p (d h) -> p d h", h=H),
                             wqkv[:, C:2 * C].rearrange("p (h d) -> p d h", h=H)).then_inc(wqk_done, 1)

            def copy_x(b, par):
                pool.tensor_copy(xc[:, par, :], xnT[:, bass.ds(b * T, T)]).then_inc(xc_done, 1)

            for b in range(NB):
                t = TB * b + TB - 1
                pool.wait_ge(rstd_done, b + 1)
                pool.tensor_scalar(xn[:, t, :], xt[:, t, :], mv[:, t, 0:1], rstd[:, t:t + 1],
                                   ALU.subtract, ALU.mult).then_inc(xn_last_done, 1)

            pool.wait_ge(xn_done, NB)
            pool.wait_ge(xn_last_done, NB)
            pool.wait_ge(slots_done, 1)
            pool.wait_ge(zero_stored, 16)
            for t in range(NT):
                pool.indirect_dma_start(xs_dram, bass.IndirectOffsetOnAxis(ap=slot[:, t:t + 1], axis=0),
                                        xn[:, t, :], None).then_inc(scattered, 16)

            def store_tile(q, r):
                pool.wait_ge(ye_done, FR * q + r + 1)
                pool.sem_inc(pool_passed, 1)
                pool.dma_start(ys_dram[bass.ds((FR * q + r) * P, P), :], yst[:, r, :]).then_inc(ys_stored[r], 16)

            sorted_tiles(pool, store_tile)
            for r in range(FR):
                pool.wait_ge(ys_stored[r], 16 * (NST // FR))
            pool.wait_ge(gate_done, 1)
            pool.wait_ge(small_loaded, 16 * N_SMALL)

            pool.sem_inc(base_done, ONE)

            def pool_at(b, half, par, pos):
                if pos == XC_AT and has(b + 2):
                    pool.wait_ge(v_ps, b + 1)
                    pool.sem_inc(pool_passed, 1)
                    copy_x(b + 2, par)
                for k in range(NG * TB):
                    if pos != ENDS[k] - 1:
                        continue
                    sb_ = k % TB
                    w = T - P * sb_
                    p = probs[:, P_AT[sb_]:P_AT[sb_] + G * w].rearrange("p (h w) -> p h w", h=G)[:, :, 0:P]
                    pool.wait_ge(exp_done, ST_RING + STEPS * b + ENDS[k])
                    pool.sem_inc(pool_passed, 1)
                    pool.affine_select(out=p, in_=p, compare_op=ALU.is_ge, fill=0.0, base=0,
                                       pattern=[[0, G], [1, P]], channel_multiplier=-1).then_inc(p_masked, 1)
                if pos == SLOTS_AT:
                    pool.wait_ge(base_done, b + 1)
                    pool.sem_inc(pool_passed, 1)
                    pool.tensor_copy(slot_cur[:, par, :], slot[:, bass.ds(TB * b, TB)]).then_inc(idx_copied, 1)
                if pos in GATHER_AT:
                    t = GATHER_AT.index(pos)
                    if t == 0:
                        pool.wait_ge(idx_copied, b + 1)
                        pool.sem_inc(pool_passed, 1)
                    pool.indirect_dma_start(ysg[:, par, t, :], None, ys_dram,
                                            bass.IndirectOffsetOnAxis(ap=slot_cur[:, par, t:t + 1], axis=0)
                                            ).then_inc(gathered[par], 16)
                if pos == GATED_AT:
                    pool.wait_ge(gathered[par], 16 * TB * (half + 1))
                    pool.tensor_tensor(ysg[:, par], ysg[:, par],
                                       gate[:, bass.ds(TB * b, TB)].unsqueeze(2).broadcast_to([P, TB, C]),
                                       ALU.mult).then_inc(gated, 1)
                if pos == BIASED_AT:
                    pool.wait_ge(out_done, b + 1)
                    pool.tensor_tensor(base[:, par], xt[:, bass.ds(TB * b, TB), :],
                                       bpb[:].unsqueeze(1).broadcast_to([P, TB, C]), ALU.add).then_inc(biased, 1)
                if pos == BASE_AT:
                    pool.wait_ge(gated, b + 1)
                    pool.wait_ge(biased, b + 1)
                    pool.tensor_tensor(base[:, par], base[:, par], ysg[:, par], ALU.add).then_inc(base_done, 1)

            timeline(pool, pool_at)

        @block.tensor
        def _(pe):
            pe.sem_inc(pv_done, P_RING)
            pe.sem_inc(yT_back, Y_RING)
            pe.sem_inc(y2_ps, ONE)
            pe.sem_inc(proj_ps, ONE)
            pe.wait_ge(const_loaded, 16 * N_CONST)

            def logits(b):
                pe.wait_ge(xnT_done, b + 1)
                for t in range(TB * b, TB * (b + 1)):
                    last = pe.matmul(ps[:, 2, t * E:(t + 1) * E], xnT[:, t * P:(t + 1) * P], wrt[:],
                                     start=True, stop=True)
                last.then_inc(logits_ps, 1)

            def project_qk(b, par, s, bank=MISC):
                pe.matmul(ps[:, bank, :], wqk_dh[:, s, :], xc[:, par, :], start=True, stop=True).then_inc(qk_ps, 1)

            def project_first(b):
                pe.wait_ge(wqk_done, 2)
                pe.wait_ge(xc_done, b + 1)
                if b:
                    pe.wait_ge(qk_left, 2 * b)
                for s in range(2):
                    project_qk(b, b, s, QK_BANK[s])

            for b in range(NB):
                pe.wait_ge(xn_done, b + 1)
                pe.wait_ge(xn_last_done, b + 1)
                if b >= 2:
                    pe.wait_ge(xnT_done, b - 1)
                for t in range(TB):
                    last = pe.transpose(ps[:, b % 2, t * P:(t + 1) * P], xn[:, TB * b + t, :], ident[:])
                last.then_inc(xnT_ps, 1)
                if b:
                    if b == 1:
                        pe.wait_ge(proj_loaded, 16 * N_PROJ)
                    logits(b - 1)
            logits(NB - 1)
            project_first(0)
            pe.wait_ge(small_loaded, 16 * N_SMALL)
            pe.transpose(ps[:, 3, 0:E * IC], b1r[:], ident[0:E * IC, 0:E * IC]).then_inc(b1_ps, 1)

            def project_v(b, par):
                for t in range(TB):
                    last = pe.matmul(ps[:, MISC, t * P:(t + 1) * P], xc[:, par, t * P:(t + 1) * P],
                                     wqkv[:, 2 * C:3 * C], start=True, stop=True)
                last.then_inc(v_ps, 1)

            def score_unit(b, half, par, g, u):
                tb, h0, nh = UNITS[u]
                w = P * (tb + 1)
                step = 2 * T // nh
                at = 64 * par
                if u == 0 and g == 0:
                    pe.wait_ge(stack_loaded[par], 16 * STACK_DMAS * (half + 1))
                pe.wait_ge(mx_done, NU * (NG * b + g) + u + 1)
                two = ps[:, S_BANK[u % 2]:S_BANK[u % 2] + 2, :].rearrange("p a t -> p (a t)")
                for n in range(nh):
                    h = G * g + h0 + n
                    pe.matmul(two[:, n * step:n * step + w],
                              stack[at:at + N_SCORE, 0, h, tb * P:(tb + 1) * P],
                              stack[at:at + N_SCORE, 1, h, 0:w], start=True, stop=False)
                    last = pe.matmul(two[:, n * step + w - P:n * step + w], ident_b, mask_b,
                                     start=False, stop=True)
                last.then_inc(s_ps, 1)

            def guard_back(b, pair):
                pe.wait_ge(mx_done, S_RING + NU * (NG * b + 2 * pair + 2))
                for tb in range(TB):
                    last = pe.matmul(ps[32 * tb:32 * tb + H // 2, MISC, 0:P],
                                     mx[:, tb, pair * H // 2:(pair + 1) * H // 2], ident[:],
                                     start=True, stop=True)
                last.then_inc(guard_ps, 1)

            pe.wait_ge(onehot_done, 1)
            pe.wait_ge(b1_done, 1)
            oh2 = ohb[:].rearrange("p n e -> p (n e)")
            pe.matmul(ps[:, 3, 0:NT * E], tri_b, oh2, start=True, stop=True)
            pe.matmul(ps[:, 3, NT * E:2 * NT * E], ones_b, oh2, start=True, stop=True).then_inc(count_ps, 1)
            project_first(1)
            project_v(0, 0)
            pe.wait_ge(slots_done, 1)
            for g in range(LEAD):
                for u in range(NU):
                    score_unit(0, 0, 0, g, u)
                if g == 1:
                    pe.wait_ge(v_done, 1)
                    guard_back(0, 0)

            def tile_transpose(q, r):
                n = FR * q + r
                pe.wait_ge(xs_loaded[r], 16 * (q + 1))
                if not first(q):
                    pe.wait_ge(ye_done, n - FR + 1)
                pe.transpose(ps[:, r, 0:P], xst[:, r, :], ident[:]).then_inc(xsT_ps, 1)

            def tile_up(q, r):
                n = FR * q + r
                pe.wait_ge(xsT_done, n + 1)
                pe.wait_ge(wcur_done, n + 1)
                if not first(q):
                    pe.wait_ge(hid_done, IC * (n - FR + 1))
                for i in range(IC):
                    last = pe.matmul(ps[:, 3 + r, i * P:(i + 1) * P],
                                     wcur[:, r, W1_AT + i * P:W1_AT + (i + 1) * P], xsT[:, r, :],
                                     start=True, stop=True)
                last.then_inc(hid_ps, 1)

            def tile_down(q, r):
                for i in range(IC):
                    pe.wait_ge(hid_done, IC * (FR * q + r) + i + 1)
                    last = pe.matmul(ps[:, r, P:P + C], hid[:, r, i, :],
                                     wcur[:, r, W2_AT + i * C:W2_AT + (i + 1) * C],
                                     start=(i == 0), stop=(i == IC - 1))
                last.then_inc(ye_ps, 1)

            def tile_step(q, r):
                tile_up(q, r)
                if not (final(q) and r == FR - 1):
                    tile_transpose(q + 1 if r == FR - 1 else q, (r + 1) % FR)
                if not (first(q) and r == 0):
                    tile_down(q - 1 if r == 0 else q, (r - 1) % FR)

            pe.wait_ge(mx_done, S_RING + NU * LEAD)
            tile_transpose(0, 0)
            sorted_tiles(pe, tile_step)
            tile_down(NST // FR - 1, FR - 1)
            pe.wait_ge(ye_done, NST)
            pe.wait_ge(qk_left, 4)
            pe.wait_ge(consts_made, 1)

            def pe_at(b, half, par, pos):
                at = 64 * par
                if pos < STEPS:
                    g, sb_, h0, nh = CHUNKS[pos]
                    w = T - P * sb_
                    if pos % (2 * GSTEPS) == 0:
                        pe.wait_ge(guard_loaded, 16 * (2 * b + 1 + pos // (2 * GSTEPS)))
                    pe.wait_ge(exp_done, STEPS * b + pos + 1)
                    for m in range(nh):
                        h = G * g + h0 + m
                        last = pe.matmul(ps[:, ST_BANK[pos % 2], m * w:(m + 1) * w],
                                         stack[at:at + N_STACK, 1, h, P * sb_:P * (sb_ + 1)],
                                         stack[at:at + N_STACK, 0, h, P * sb_:T], start=True, stop=True)
                    last.then_inc(st_ps, 1)
                unit = max_group(b, half, par, pos)
                if unit:
                    score_unit(*unit)
                for k in range(NG * TB):
                    if pos != weigh_at(k):
                        continue
                    g, sb_ = divmod(k, TB)
                    w = T - P * sb_
                    pe.wait_ge(p_masked, NG * TB * b + k + 1)
                    if sb_ == 0 and g % 2 == 0:
                        pe.wait_ge(yT_copied, NY * b + g // 2 + 1)
                        if g == 0:
                            pe.wait_ge(v_done, b + 1)
                    for m in range(G):
                        last = pe.matmul(ps[32 * m:32 * m + V2, PV_BANK, P * sb_:T],
                                         vt[:, par, sb_, G * g + m, :],
                                         probs[:, P_AT[sb_] + m * w:P_AT[sb_] + (m + 1) * w],
                                         start=(sb_ == 0 and g % 2 == 0),
                                         stop=(sb_ == TB - 1 and g % 2 == 1))
                    last.then_inc(pv_done, 1)

                pair = guard_pair(b, half, par, pos)
                if pair:
                    if pair[3] == 1:
                        pe.wait_ge(out_done, b + 1)
                    elif has(b + 2):
                        pe.wait_ge(qk_left, 2 * (b + 2) + 2)
                    else:
                        pe.wait_ge(y_norm, NY * b + 1)
                    guard_back(pair[0], pair[3])
                if pos == V_AT and has(b + 1):
                    pe.wait_ge(guard_left, 2 * b + 2)
                    project_v(b + 1, 1 - par)
                if pos == Q_AT and has(b + 2):
                    pe.wait_ge(v_done, b + 2)
                    pe.wait_ge(xc_done, b + 3)
                    project_qk(b + 2, par, 0)
                if pos == K_AT and has(b + 2):
                    pe.wait_ge(y_norm, NY * b + 1)
                    project_qk(b + 2, par, 1)
                for y in range(NY):
                    if pos != y_back_at(y):
                        continue
                    if y == 0 and has(b + 2):
                        pe.wait_ge(qk_left, 2 * (b + 2) + 1)
                    elif y == 0 and has(b + 1):
                        pe.wait_ge(v_done, b + 2)
                    elif y == 0:
                        pe.wait_ge(guard_left, 2 * b + 2)
                    elif has(b + 1):
                        pe.wait_ge(guard_left, 2 * b + 3)
                    else:
                        pe.wait_ge(y_norm, NY * b + 1)
                    pe.wait_ge(yT_copied, ONE + NY * b + y + 1)
                    for t in range(TB):
                        last = pe.matmul(ps[:, MISC, t * G * V2:(t + 1) * G * V2],
                                         yTs[:, y, t * P:(t + 1) * P],
                                         ident[:].rearrange("p (m r) -> p m r", m=G)[:, :, 0:V2],
                                         start=True, stop=True)
                    last.then_inc(yT_back, 1)
                if pos == Y2_AT:
                    pe.wait_ge(y_norm, NY * b + NY)
                    for t in range(TB):
                        last = pe.transpose(ps[:, MISC, t * P:(t + 1) * P], yn[:, t, :], ident[:])
                    last.then_inc(y2_ps, 1)
                if pos == PROJ_AT:
                    pe.wait_ge(y2_copied, b + 1)
                    for t in range(TB):
                        last = pe.matmul(ps[:, MISC, t * C:(t + 1) * C], yn2[:, t * P:(t + 1) * P], wpj[:],
                                         start=True, stop=True)
                    last.then_inc(proj_ps, 1)

            timeline(pe, pe_at)


def top_bits(a):
    import numpy as np

    bits = np.ascontiguousarray(a, np.float32).view(np.uint32)
    kept = (bits & np.uint32(0xFFFF0000)).view(np.float32)
    return (bits >> np.uint32(16)).astype(np.uint16), (a - kept).astype(np.float32)


def shape_constants():
    import numpy as np

    pos = np.arange(T)
    slopes = (2.0 ** (-(8.0 / H) * np.arange(1, H + 1))).astype(np.float32)
    left = slopes[:, None] * pos[None, :].astype(np.float32)
    alibi = []
    for _ in range(N_ALIBI):
        part, left = top_bits(left)
        alibi.append(part)
    one = top_bits(np.ones((H, T), np.float32))[0]
    block = np.arange(CM)[:, None, None]
    in_block = pos[None, None] // (T // CM)
    before = top_bits(np.broadcast_to(np.where(in_block < block, -BIG, 0.0), (CM, H, T)).astype(np.float32))[0]
    inside = top_bits(np.broadcast_to(in_block == block, (CM, H, T)).astype(np.float32))[0]
    stack_q = np.concatenate([np.stack([one] * N_ALIBI), before])
    stack_k = np.concatenate([np.stack(alibi), inside, np.stack([one] * 3)])
    r = np.arange(P)
    bf = np.stack([np.eye(P), np.where(r[None] > r[:, None], -BIG, 0.0), r[:, None] < r[None], np.ones((P, P))], 1)
    return {"c_ident": np.eye(P, dtype=np.float32), "c_bf": top_bits(bf.astype(np.float32))[0],
            "c_stack_q": stack_q, "c_stack_k": stack_k}


_INS = ["L0_attn_x", "L0_attn_w_attn", "L0_attn_b_attn", "L0_attn_w_proj", "L0_attn_b_proj", "L0_ffn_w1",
        "L0_ffn_b1", "L0_ffn_w2", "L0_ffn_b2", "L0_ffn_wr", "L0_ffn_br"]


def kernel(**inputs):
    import numpy as np
    import concourse.bacc as bacc
    from concourse.bass_utils import run_bass_kernel_spmd

    nc = bacc.Bacc("TRN2", target_bir_lowering=False, num_devices=1)
    arrays = {name: np.ascontiguousarray(inputs[name]) for name in _INS}
    arrays.update(shape_constants())
    args = [nc.dram_tensor(name, a.shape, mybir.dt.from_np(a.dtype), kind="ExternalInput").ap()
            for name, a in arrays.items()]
    out = nc.dram_tensor("out", (NB, T, C), F32, kind="ExternalOutput").ap()
    block_kernel(nc, *args, out)
    return run_bass_kernel_spmd(nc, [arrays], core_ids=[0]).results[0]["out"]
```
